# Optimizing a Trainium2 kernel written in Bass

```python
import numpy as np
import jax
import jax.numpy as jnp

def _softmax(x, axis=-1):
    return jax.nn.softmax(x, axis=axis)
def _gelu(x):
    return jax.nn.gelu(x, approximate=True)
def _silu(x):
    return jax.nn.silu(x)
def _sigmoid(x):
    return jax.nn.sigmoid(x)
def _layernorm(x, axis=-1, eps=1e-5):
    m = jnp.mean(x, axis=axis, keepdims=True)
    v = jnp.var(x, axis=axis, keepdims=True)
    return (x - m) / jnp.sqrt(v + eps)
def _scatter_add(tgt, idx, src, axis=0):
    return tgt.at[idx].add(src)
def _segment_sum(src, seg, n):
    return jax.ops.segment_sum(src, seg, n)

kernel_name = 'mk_metaformer_d1_conv_nchw256_cf4554'

def setup_inputs(seed: int = 0):
    np.random.seed(seed)
    _w = jnp.asarray
    def _rec_inputs():
        import jax
        import jax.numpy as jnp
        _gk = jax.random.key(seed)
        x = -0.0005207 + 1.001 * jax.random.normal(jax.random.fold_in(_gk, 1), (8, 256, 32, 32), jnp.float32)
        return x
    x = _rec_inputs()
    def _L0_conv_setup():
        import jax, jax.numpy as jnp
        import numpy as np
        from jax import lax
        IH, IW = (32, 32)
        N = IH * IW
        C = 256
        HEADS = 8
        DH = C // HEADS
        SCALE = 32 ** (-0.5)
        EPS = 1e-06

        def _rel_index():
            coords = np.stack(np.meshgrid(np.arange(IH), np.arange(IW), indexing='ij')).reshape(2, -1)
            rel = coords[:, :, None] - coords[:, None, :]
            rel[0] += IH - 1
            rel[1] += IW - 1
            rel[0] *= 2 * IW - 1
            return jnp.asarray(rel.sum(0).reshape(-1))
        REL_IDX = _rel_index()

        def _conv3(x, W):
            return lax.conv_general_dilated(x, W, (1, 1), 'SAME', dimension_numbers=('NCHW', 'OIHW', 'NCHW'))

        def _proj(x, W, g, b):
            y = _conv3(x, W)
            m = jnp.mean(y, axis=(1, 2, 3), keepdims=True)
            v = jnp.var(y, axis=(1, 2, 3), keepdims=True)
            y = (y - m) * lax.rsqrt(v + EPS) * g[None, :, None, None] + b[None, :, None, None]
            y = jax.nn.gelu(y, approximate=False)
            B = y.shape[0]
            return y.reshape(B, HEADS, DH, N).transpose(0, 1, 3, 2)
        key = jax.random.key(seed)
        ks = jax.random.split(key, 8)
        s = 0.02
        return {'x': jax.random.normal(ks[0], (8, C, IH, IW), dtype=jnp.float32), 'Wq': jax.random.normal(ks[1], (C, C, 3, 3), dtype=jnp.float32) * s, 'gq': jnp.ones((C,), jnp.float32), 'bq': jnp.zeros((C,), jnp.float32), 'Wk': jax.random.normal(ks[2], (C, C, 3, 3), dtype=jnp.float32) * s, 'gk': jnp.ones((C,), jnp.float32), 'bk': jnp.zeros((C,), jnp.float32), 'Wv': jax.random.normal(ks[3], (C, C, 3, 3), dtype=jnp.float32) * s, 'gv': jnp.ones((C,), jnp.float32), 'bv': jnp.zeros((C,), jnp.float32), 'bias_table': jax.random.normal(ks[4], ((2 * IH - 1) * (2 * IW - 1), HEADS), dtype=jnp.float32) * s, 'Wout': jax.random.normal(ks[5], (C, C, 1, 1), dtype=jnp.float32) * s, 'bout': jnp.zeros((C,), jnp.float32)}
    _L0_conv_all = _L0_conv_setup()
    _L0_conv_in = {k: v for k, v in _L0_conv_all.items() if k in ('Wq', 'gq', 'bq', 'Wk', 'gk', 'bk', 'Wv', 'gv', 'bv', 'bias_table', 'Wout', 'bout', )}
    del _L0_conv_all

    def _L0_ffn_setup():
        import jax, jax.numpy as jnp
        import numpy as np
        B, N, D = (16, 4096, 256)
        NUM_EXPERTS, TOP_K, HEADS = (4, 2, 4)
        N_EDGES = 1048576
        LN_EPS = 1e-05

        def _layernorm(x, g, b):
            mu = x.mean(-1, keepdims=True)
            var = ((x - mu) ** 2).mean(-1, keepdims=True)
            return (x - mu) * jax.lax.rsqrt(var + LN_EPS) * g + b

        def _forward(x, edge_index, W_gat, att_src, att_dst, b_gat, ln_gamma, ln_beta, W1, b1, W2, b2):
            Bc, Nc, Dc = x.shape
            M = Bc * Nc
            x_flat = x.reshape(M, Dc)
            h = (x_flat @ W_gat).reshape(M, HEADS, NUM_EXPERTS)
            loops = jnp.arange(M, dtype=edge_index.dtype)
            src = jnp.concatenate([edge_index[0], loops])
            dst = jnp.concatenate([edge_index[1], loops])
            a_src = (h * att_src).sum(-1)
            a_dst = (h * att_dst).sum(-1)
            e = jax.nn.leaky_relu(a_src[src] + a_dst[dst], negative_slope=0.2)
            e_max = jax.ops.segment_max(e, dst, num_segments=M)
            ee = jnp.exp(e - e_max[dst])
            denom = jax.ops.segment_sum(ee, dst, num_segments=M)
            alpha = ee / (denom[dst] + 1e-16)
            msg = h[src] * alpha[:, :, None]
            agg = jax.ops.segment_sum(msg, dst, num_segments=M).reshape(M, HEADS * NUM_EXPERTS) + b_gat
            scores = _layernorm(agg, ln_gamma, ln_beta).reshape(M, HEADS, NUM_EXPERTS).mean(1)
            scores = scores.reshape(Bc, Nc, NUM_EXPERTS)
            topk_s, topk_i = jax.lax.top_k(scores, TOP_K)
            w = jax.nn.softmax(topk_s, axis=-1)
            out = jnp.zeros_like(x)
            for ei in range(NUM_EXPERTS):
                g = jnp.where(topk_i == ei, w, 0.0).sum(-1)
                hh = jax.nn.gelu(x @ W1[ei] + b1[ei], approximate=False)
                out = out + g[..., None] * (hh @ W2[ei] + b2[ei])
            return out
        key = jax.random.key(seed)
        ks = jax.random.split(key, 8)
        s = 0.05
        return {'x': jax.random.normal(ks[0], (B, N, D), jnp.float32), 'W_gat': jax.random.normal(ks[1], (D, HEADS * NUM_EXPERTS), jnp.float32) * s, 'att_src': jax.random.normal(ks[2], (HEADS, NUM_EXPERTS), jnp.float32) * s, 'att_dst': jax.random.normal(ks[3], (HEADS, NUM_EXPERTS), jnp.float32) * s, 'b_gat': jnp.zeros((HEADS * NUM_EXPERTS,), jnp.float32), 'ln_gamma': jnp.ones((HEADS * NUM_EXPERTS,), jnp.float32), 'ln_beta': jnp.zeros((HEADS * NUM_EXPERTS,), jnp.float32), 'W1': jax.random.normal(ks[4], (NUM_EXPERTS, D, 2 * D), jnp.float32) * s, 'b1': jnp.zeros((NUM_EXPERTS, 2 * D), jnp.float32), 'W2': jax.random.normal(ks[5], (NUM_EXPERTS, 2 * D, D), jnp.float32) * s, 'b2': jnp.zeros((NUM_EXPERTS, D), jnp.float32), 'edge_index': jax.random.randint(ks[6], (2, N_EDGES), 0, B * N, jnp.int32)}
    _L0_ffn_all = _L0_ffn_setup()
    _L0_ffn_in = {k: v for k, v in _L0_ffn_all.items() if k in ('W_gat', 'att_src', 'att_dst', 'b_gat', 'ln_gamma', 'ln_beta', 'W1', 'b1', 'W2', 'b2', 'edge_index', )}
    del _L0_ffn_all

    return {
        "x": x,
        "L0_conv_Wq": _L0_conv_in["Wq"],
        "L0_conv_gq": _L0_conv_in["gq"],
        "L0_conv_bq": _L0_conv_in["bq"],
        "L0_conv_Wk": _L0_conv_in["Wk"],
        "L0_conv_gk": _L0_conv_in["gk"],
        "L0_conv_bk": _L0_conv_in["bk"],
        "L0_conv_Wv": _L0_conv_in["Wv"],
        "L0_conv_gv": _L0_conv_in["gv"],
        "L0_conv_bv": _L0_conv_in["bv"],
        "L0_conv_bias_table": _L0_conv_in["bias_table"],
        "L0_conv_Wout": _L0_conv_in["Wout"],
        "L0_conv_bout": _L0_conv_in["bout"],
        "L0_ffn_W_gat": _L0_ffn_in["W_gat"],
        "L0_ffn_att_src": _L0_ffn_in["att_src"],
        "L0_ffn_att_dst": _L0_ffn_in["att_dst"],
        "L0_ffn_b_gat": _L0_ffn_in["b_gat"],
        "L0_ffn_ln_gamma": _L0_ffn_in["ln_gamma"],
        "L0_ffn_ln_beta": _L0_ffn_in["ln_beta"],
        "L0_ffn_W1": _L0_ffn_in["W1"],
        "L0_ffn_b1": _L0_ffn_in["b1"],
        "L0_ffn_W2": _L0_ffn_in["W2"],
        "L0_ffn_b2": _L0_ffn_in["b2"],
        "L0_ffn_edge_index": _L0_ffn_in["edge_index"],
    }

def reference(x, L0_conv_Wq, L0_conv_gq, L0_conv_bq, L0_conv_Wk, L0_conv_gk, L0_conv_bk, L0_conv_Wv, L0_conv_gv, L0_conv_bv, L0_conv_bias_table, L0_conv_Wout, L0_conv_bout, L0_ffn_W_gat, L0_ffn_att_src, L0_ffn_att_dst, L0_ffn_b_gat, L0_ffn_ln_gamma, L0_ffn_ln_beta, L0_ffn_W1, L0_ffn_b1, L0_ffn_W2, L0_ffn_b2, L0_ffn_edge_index):
    import jax
    import jax.numpy as jnp
    def _L0_conv_ref(x, Wq, gq, bq, Wk, gk, bk, Wv, gv, bv, bias_table, Wout, bout):
        import jax, jax.numpy as jnp
        import numpy as np
        from jax import lax
        IH, IW = (32, 32)
        N = IH * IW
        C = 256
        HEADS = 8
        DH = C // HEADS
        SCALE = 32 ** (-0.5)
        EPS = 1e-06

        def _rel_index():
            coords = np.stack(np.meshgrid(np.arange(IH), np.arange(IW), indexing='ij')).reshape(2, -1)
            rel = coords[:, :, None] - coords[:, None, :]
            rel[0] += IH - 1
            rel[1] += IW - 1
            rel[0] *= 2 * IW - 1
            return jnp.asarray(rel.sum(0).reshape(-1))
        REL_IDX = _rel_index()

        def _conv3(x, W):
            return lax.conv_general_dilated(x, W, (1, 1), 'SAME', dimension_numbers=('NCHW', 'OIHW', 'NCHW'))

        def _proj(x, W, g, b):
            y = _conv3(x, W)
            m = jnp.mean(y, axis=(1, 2, 3), keepdims=True)
            v = jnp.var(y, axis=(1, 2, 3), keepdims=True)
            y = (y - m) * lax.rsqrt(v + EPS) * g[None, :, None, None] + b[None, :, None, None]
            y = jax.nn.gelu(y, approximate=False)
            B = y.shape[0]
            return y.reshape(B, HEADS, DH, N).transpose(0, 1, 3, 2)
        B = x.shape[0]
        q = _proj(x, Wq, gq, bq)
        k = _proj(x, Wk, gk, bk)
        v = _proj(x, Wv, gv, bv)
        dots = jnp.einsum('bhnd,bhmd->bhnm', q, k) * SCALE
        bias = bias_table[REL_IDX].reshape(N, N, HEADS).transpose(2, 0, 1)[None]
        attn = jax.nn.softmax(dots + bias, axis=-1)
        out = jnp.einsum('bhnm,bhmd->bhnd', attn, v)
        out = out.transpose(0, 2, 1, 3).reshape(B, N, C).transpose(0, 2, 1).reshape(B, C, IH, IW)
        out = jnp.einsum('oc,bchw->bohw', Wout[:, :, 0, 0], out) + bout[None, :, None, None]
        return out

    def _L0_ffn_ref(x, W_gat, att_src, att_dst, b_gat, ln_gamma, ln_beta, W1, b1, W2, b2, edge_index):
        import jax, jax.numpy as jnp
        import numpy as np
        B, N, D = (16, 4096, 256)
        NUM_EXPERTS, TOP_K, HEADS = (4, 2, 4)
        N_EDGES = 1048576
        LN_EPS = 1e-05

        def _layernorm(x, g, b):
            mu = x.mean(-1, keepdims=True)
            var = ((x - mu) ** 2).mean(-1, keepdims=True)
            return (x - mu) * jax.lax.rsqrt(var + LN_EPS) * g + b

        def _forward(x, edge_index, W_gat, att_src, att_dst, b_gat, ln_gamma, ln_beta, W1, b1, W2, b2):
            Bc, Nc, Dc = x.shape
            M = Bc * Nc
            x_flat = x.reshape(M, Dc)
            h = (x_flat @ W_gat).reshape(M, HEADS, NUM_EXPERTS)
            loops = jnp.arange(M, dtype=edge_index.dtype)
            src = jnp.concatenate([edge_index[0], loops])
            dst = jnp.concatenate([edge_index[1], loops])
            a_src = (h * att_src).sum(-1)
            a_dst = (h * att_dst).sum(-1)
            e = jax.nn.leaky_relu(a_src[src] + a_dst[dst], negative_slope=0.2)
            e_max = jax.ops.segment_max(e, dst, num_segments=M)
            ee = jnp.exp(e - e_max[dst])
            denom = jax.ops.segment_sum(ee, dst, num_segments=M)
            alpha = ee / (denom[dst] + 1e-16)
            msg = h[src] * alpha[:, :, None]
            agg = jax.ops.segment_sum(msg, dst, num_segments=M).reshape(M, HEADS * NUM_EXPERTS) + b_gat
            scores = _layernorm(agg, ln_gamma, ln_beta).reshape(M, HEADS, NUM_EXPERTS).mean(1)
            scores = scores.reshape(Bc, Nc, NUM_EXPERTS)
            topk_s, topk_i = jax.lax.top_k(scores, TOP_K)
            w = jax.nn.softmax(topk_s, axis=-1)
            out = jnp.zeros_like(x)
            for ei in range(NUM_EXPERTS):
                g = jnp.where(topk_i == ei, w, 0.0).sum(-1)
                hh = jax.nn.gelu(x @ W1[ei] + b1[ei], approximate=False)
                out = out + g[..., None] * (hh @ W2[ei] + b2[ei])
            return out
        return _forward(x, edge_index, W_gat, att_src, att_dst, b_gat, ln_gamma, ln_beta, W1, b1, W2, b2)

    def _gn(v, G=32, eps=1e-5):
        B_, C_, H_, W_ = v.shape
        g = v.reshape(B_, G, C_ // G, H_, W_)
        m = jnp.mean(g, axis=(2, 3, 4), keepdims=True)
        s = jnp.var(g, axis=(2, 3, 4), keepdims=True)
        return ((g - m) / jnp.sqrt(s + eps)).reshape(v.shape)

    def _ln_c(v, eps=1e-6):
        m = jnp.mean(v, axis=1, keepdims=True)
        s = jnp.var(v, axis=1, keepdims=True)
        return (v - m) / jnp.sqrt(s + eps)

    def _ln_t(v, eps=1e-5):
        m = jnp.mean(v, axis=-1, keepdims=True)
        s = jnp.var(v, axis=-1, keepdims=True)
        return (v - m) / jnp.sqrt(s + eps)

    def _to_tokens(v):
        B_, C_, H_, W_ = v.shape
        return v.reshape(B_, C_, H_ * W_).transpose(0, 2, 1)
    def _from_tokens(t, like):
        B_, C_, H_, W_ = like.shape
        return t.transpose(0, 2, 1).reshape(B_, C_, H_, W_)

    x = x + _L0_conv_ref(_ln_c(x), L0_conv_Wq, L0_conv_gq, L0_conv_bq, L0_conv_Wk, L0_conv_gk, L0_conv_bk, L0_conv_Wv, L0_conv_gv, L0_conv_bv, L0_conv_bias_table, L0_conv_Wout, L0_conv_bout)
    t = _to_tokens(x)
    t = t + _L0_ffn_ref(_ln_t(t), L0_ffn_W_gat, L0_ffn_att_src, L0_ffn_att_dst, L0_ffn_b_gat, L0_ffn_ln_gamma, L0_ffn_ln_beta, L0_ffn_W1, L0_ffn_b1, L0_ffn_W2, L0_ffn_b2, L0_ffn_edge_index)
    x = _from_tokens(t, x)
    return x


_drawn_inputs = setup_inputs


def setup_inputs(seed=0):
    import zlib

    import numpy as np

    out = dict(_drawn_inputs(seed))
    spreads = {'L0_conv_gq': (1.0, 0.6),
     'L0_conv_bq': (0.0, 2.0),
     'L0_conv_gk': (1.0, 0.6),
     'L0_conv_bk': (0.0, 2.0),
     'L0_conv_gv': (1.0, 0.55),
     'L0_conv_bv': (0.0, 0.478),
     'L0_conv_bout': (0.0, 0.1),
     'L0_ffn_b_gat': (0.0, 0.1),
     'L0_ffn_ln_gamma': (1.0, 0.2),
     'L0_ffn_ln_beta': (0.0, 0.1),
     'L0_ffn_b1': (0.0, 0.1),
     'L0_ffn_b2': (0.0, 0.1)}
    factors = {'L0_conv_Wq': 8.0,
     'L0_conv_Wk': 8.0,
     'L0_conv_Wv': 7.188,
     'L0_conv_bias_table': 60.733,
     'L0_ffn_att_src': 8.0,
     'L0_ffn_att_dst': 8.0}
    for name, (base, spread) in spreads.items():
        noise = np.random.default_rng([zlib.crc32(name.encode()), seed]).standard_normal(out[name].shape)
        drawn = base * np.exp(spread * noise) if base else spread * noise
        out[name] = jnp.asarray(drawn.astype(out[name].dtype))
    for name, factor in factors.items():
        out[name] = (out[name] * factor).astype(out[name].dtype)
    return out
```

```python
from contextlib import ExitStack

import numpy as np

import concourse.bass as bass
from concourse import mybir

F32 = mybir.dt.float32
BF16 = mybir.dt.bfloat16
I32 = mybir.dt.int32
ALU = mybir.AluOpType
ACT = mybir.ActivationFunctionType
AX = mybir.AxisListType

P = 128
B, C, IH, IW = 8, 256, 32, 32
N = IH * IW
CT = C // P
HALF = 512
HALVES = N // HALF
HEADS, DH = 8, 32
SCALE = DH ** -0.5
PADW = IW + 2
TAPS = 9
M = B * N
BIG = 3.0e38


class Space:

    def __init__(self, nc, ctx, stage):
        self.nc, self.ctx, self.stage = nc, ctx, stage

    def sb(self, name, shape, dt=F32):
        return self.ctx.enter_context(self.nc.sbuf_tensor(f"{self.stage}_{name}", shape, dt))

    def ps(self, name, shape, dt=F32):
        return self.ctx.enter_context(self.nc.psum_tensor(f"{self.stage}_{name}", shape, dt))

    def sem(self, name):
        return self.ctx.enter_context(self.nc.semaphore(f"{self.stage}_{name}"))


def project(nc, x, weights, gains, shifts, qkv):
    EPS_LN = EPS_PROJ = 1e-6
    GROUPS = 3 * CT * HALVES
    with ExitStack() as ctx:
        s = Space(nc, ctx, "project")
        w = [s.sb(f"w{p}", [P, CT, TAPS, C]) for p in range(3)]
        gain = s.sb("gain", [P, 3, CT])
        shift = s.sb("shift", [P, 3, CT])
        ones_c = s.sb("ones_c", [P, P])
        ones_p = s.sb("ones_p", [P, P])
        x_in = [s.sb(f"x_in{i}", [P, CT, N]) for i in range(2)]
        xc = s.sb("xc", [P, CT, N])
        sq = s.sb("sq", [P, CT, N])
        stdev = s.sb("stdev", [P, N])
        rstd = s.sb("rstd", [P, N])
        eps = s.sb("eps", [P, 1])
        xn = [s.sb(f"xn{i}", [P, CT, IH + 2, PADW]) for i in range(2)]
        y = [s.sb(f"y{p}", [P, CT, N]) for p in range(3)]
        stats = s.sb("stats", [P, 3, CT * HALVES, 6])
        mv = s.sb("mv", [P, 3, 2])
        mean_s = s.sb("mean_s", [P, 3])
        dev = s.sb("dev", [P, 3])
        spread = s.sb("spread", [P, 3])
        y_std = s.sb("y_std", [P, 3])
        inv = s.sb("inv", [P, 3])
        a_scale = s.sb("a_scale", [P, 3, CT])
        a_prod = s.sb("a_prod", [P, 3, CT])
        a_bias = s.sb("a_bias", [P, 3, CT])
        ps_ln = s.ps("ps_ln", [P, HALVES, HALF])
        ps_conv = [s.ps(f"ps_conv{i}", [P, HALF]) for i in range(4)]
        ps_tiny = s.ps("ps_tiny", [P, 8])

        params_in, consts = s.sem("params_in"), s.sem("consts")
        x_loaded = [s.sem(f"x_loaded{i}") for i in range(2)]
        mean_ready, centered, squared = s.sem("mean_ready"), s.sem("centered"), s.sem("squared")
        var_ready, rstd_ready, xn_ready = s.sem("var_ready"), s.sem("rstd_ready"), s.sem("xn_ready")
        conv_done, conv_copied, conv_stat = s.sem("conv_done"), s.sem("conv_copied"), s.sem("conv_stat")
        aggregated, m_ready, dev_done = s.sem("aggregated"), s.sem("m_ready"), s.sem("dev_done")
        spread_ready, v_ready, inv_done = s.sem("spread_ready"), s.sem("v_ready"), s.sem("inv_done")
        scale_done, prod_done = s.sem("scale_done"), s.sem("prod_done")
        affine_ready, gelu_done, q_done = s.sem("affine_ready"), s.sem("gelu_done"), s.sem("q_done")
        scaled_from, stdev_ready, y_std_ready = s.sem("scaled_from"), s.sem("stdev_ready"), s.sem("y_std_ready")
        aggr_may = s.sem("aggr_may")
        stored = [s.sem(f"stored{p}") for p in range(3)]

        with nc.Block() as block:

            @block.sync
            def _(sp):
                for p in range(3):
                    sp.dma_start(gain[:, p, :], gains[p]).then_inc(params_in, 16)
                    sp.dma_start(shift[:, p, :], shifts[p]).then_inc(params_in, 16)
                sp.dma_start(x_in[0][:], x[0].rearrange("(c p) h w -> p c (h w)", p=P)).then_inc(x_loaded[0], 16)
                for p in range(3):
                    sp.dma_start(w[p][:], weights[p].rearrange("(c p) t o -> p c t o", p=P)).then_inc(params_in, 16)

                def image(b, i, last):
                    if not last:
                        if not (isinstance(b, int) and b == 0):
                            sp.wait_ge(centered, b)
                        nxt = b + 1
                        sp.dma_start(x_in[1 - i][:], x[bass.ds(nxt, 1)].rearrange("a (c p) h w -> p (a c) (h w)", p=P)
                                     ).then_inc(x_loaded[1 - i], 16)
                    for p in range(3):
                        sp.wait_ge(gelu_done if p else q_done, 2 * b + p if p else b + 1)
                        sp.dma_start(qkv[p, bass.ds(b, 1)].rearrange("a (c p) n -> p (a c) n", p=P), y[p][:]
                                     ).then_inc(stored[p], 16)

                image(0, 0, False)
                image(1, 1, False)
                with sp.Fori(1, B // 2 - 1) as it:
                    image(2 * it, 0, False)
                    image(2 * it + 1, 1, False)
                image(B - 2, 0, False)
                image(B - 1, 1, True)
                for p in range(3):
                    sp.wait_ge(stored[p], 16 * B)

            @block.tensor
            def _(pe):
                def mean(b, i):
                    pe.wait_ge(x_loaded[i], 16 * (b // 2) + 16 if isinstance(b, int) else 8 * (b - i) + 16)
                    if not (isinstance(b, int) and b == 0):
                        pe.wait_ge(rstd_ready, b)
                    for half in range(HALVES):
                        for c in range(CT):
                            mm = pe.matmul(ps_ln[:, half, :], ones_c[:], x_in[i][:, c, half * HALF:(half + 1) * HALF],
                                           start=c == 0, stop=c == CT - 1)
                    mm.then_inc(mean_ready, 1)

                def variance(b):
                    pe.wait_ge(squared, b + 1)
                    for half in range(HALVES):
                        for c in range(CT):
                            mm = pe.matmul(ps_ln[:, half, :], ones_c[:], sq[:, c, half * HALF:(half + 1) * HALF],
                                           start=c == 0, stop=c == CT - 1)
                    mm.then_inc(var_ready, 1)

                def over_partitions(k, p, what):
                    if what == "mean":
                        pe.wait_ge(aggregated, k + 1)
                        pe.matmul(ps_tiny[:, p:p + 1], ones_p[:], mv[:, p, 0:1], start=True, stop=True
                                  ).then_inc(m_ready, 1)
                    else:
                        pe.wait_ge(spread_ready, k + 1)
                        pe.matmul(ps_tiny[:, 4 + p:5 + p], ones_p[:], spread[:, p:p + 1], start=True, stop=True
                                  ).then_inc(v_ready, 1)

                def image(b, i, last):
                    pe.wait_ge(xn_ready, b + 1)
                    for g in range(GROUPS):
                        p, ct, half = g // 4, g // 2 % 2, g % 2
                        if not (isinstance(b, int) and b == 0 and g < 4):
                            pe.wait_ge(conv_copied, GROUPS * b + g - 3)
                        for c in range(CT):
                            for t in range(TAPS):
                                r0 = half * (IH // 2) + t // 3
                                mm = pe.matmul(ps_conv[g % 4][:], w[p][:, c, t, ct * P:(ct + 1) * P],
                                               xn[i][:, c, r0:r0 + IH // 2, t % 3:t % 3 + IW],
                                               start=c == 0 and t == 0, stop=c == CT - 1 and t == TAPS - 1)
                        mm.then_inc(conv_done, 1)
                        if g == 2 and not last:
                            mean(b + 1, 1 - i)
                        if g == 6 and not last:
                            variance(b + 1)
                        if g in (4, 8):
                            over_partitions(3 * b + p - 1, p - 1, "mean")
                        if g in (5, 9):
                            over_partitions(3 * b + p - 1, p - 1, "spread")
                    over_partitions(3 * b + 2, 2, "mean")
                    over_partitions(3 * b + 2, 2, "spread")

                pe.wait_ge(consts, 5)
                mean(0, 0)
                variance(0)
                pe.wait_ge(params_in, 16 * 9)
                image(0, 0, False)
                image(1, 1, False)
                with pe.Fori(1, B // 2 - 1) as it:
                    image(2 * it, 0, False)
                    image(2 * it + 1, 1, False)
                image(B - 2, 0, False)
                image(B - 1, 1, True)

            @block.vector
            def _(dve):
                dve.memset(ones_c[:], 1.0 / C).then_inc(consts, 1)
                dve.memset(ones_p[:], 1.0 / P).then_inc(consts, 1)
                dve.memset(eps[:], EPS_LN).then_inc(consts, 1)
                for i in range(2):
                    dve.memset(xn[i][:], 0.0).then_inc(consts, 1)

                def center(b, i):
                    dve.wait_ge(mean_ready, b + 1)
                    if not (isinstance(b, int) and b == 0):
                        dve.wait_ge(xn_ready, b)
                    dve.tensor_tensor(xc[:, 0, :], x_in[i][:, 0, :], ps_ln[:].rearrange("p a b -> p (a b)"), ALU.subtract)
                    dve.tensor_tensor(xc[:, 1, :], x_in[i][:, 1, :], ps_ln[:].rearrange("p a b -> p (a b)"), ALU.subtract
                                      ).then_inc(centered, 1)

                def normalise(b, i):
                    dve.wait_ge(stdev_ready, b + 1)
                    dve.reciprocal(rstd[:], stdev[:]).then_inc(rstd_ready, 1)
                    dve.wait_ge(rstd_ready, b + 1)
                    if not (isinstance(b, int) and b < 2):
                        dve.wait_ge(conv_done, GROUPS * (b - 1))
                    for c in range(CT):
                        op = dve.tensor_tensor(xn[i][:, c, 1:1 + IH, 1:1 + IW],
                                               xc[:, c, :].rearrange("p (h w) -> p h w", w=IW),
                                               rstd[:].rearrange("p (h w) -> p h w", w=IW), ALU.mult)
                    op.then_inc(xn_ready, 1)

                def deviation(k, p):
                    dve.wait_ge(m_ready, k + 1)
                    dve.tensor_copy(mean_s[:, p:p + 1], ps_tiny[:, p:p + 1])
                    dve.tensor_tensor(dev[:, p:p + 1], mv[:, p, 0:1], ps_tiny[:, p:p + 1], ALU.subtract
                                      ).then_inc(dev_done, 1)
                    dve.wait_ge(dev_done, k + 1)
                    dve.scalar_tensor_tensor(spread[:, p:p + 1], dev[:, p:p + 1], dev[:, p:p + 1], mv[:, p, 1:2],
                                             ALU.mult, ALU.add).then_inc(spread_ready, 1)

                def affine(k, p):
                    dve.wait_ge(y_std_ready, k + 1)
                    dve.reciprocal(inv[:, p:p + 1], y_std[:, p:p + 1]).then_inc(inv_done, 1)
                    dve.wait_ge(inv_done, k + 1)
                    dve.tensor_scalar(a_scale[:, p, :], gain[:, p, :], inv[:, p:p + 1], None, ALU.mult
                                      ).then_inc(scale_done, 1)
                    dve.wait_ge(scale_done, k + 1)
                    dve.tensor_scalar(a_prod[:, p, :], a_scale[:, p, :], mean_s[:, p:p + 1], None, ALU.mult
                                      ).then_inc(prod_done, 1)
                    dve.wait_ge(prod_done, k + 1)
                    dve.tensor_tensor(a_bias[:, p, :], shift[:, p, :], a_prod[:, p, :], ALU.subtract
                                      ).then_inc(affine_ready, 1)

                def image(b, i, last):
                    for g in range(GROUPS):
                        p = g // 4
                        ct, half = g // 2 % 2, g % 2 if p == 0 else 1 - g % 2
                        dve.wait_ge(conv_copied, GROUPS * b + g + 1)
                        dve.bn_stats(stats[:, p, g % 4, :], y[p][:, ct, half * HALF:(half + 1) * HALF]
                                     ).then_inc(conv_stat, 1)
                        if g % 4 == 3:
                            dve.wait_ge(conv_stat, GROUPS * b + g + 1)
                            dve.sem_inc(aggr_may, 1)
                            dve.bn_aggr(mv[:, p, :], stats[:, p, :, :]).then_inc(aggregated, 1)
                        if g == 3 and not last:
                            center(b + 1, 1 - i)
                        if g == 7 and not last:
                            normalise(b + 1, 1 - i)
                        if g in (4, 8):
                            deviation(3 * b + p - 1, p - 1)
                        if g in (5, 9):
                            affine(3 * b + p - 1, p - 1)
                    deviation(3 * b + 2, 2)
                    affine(3 * b + 2, 2)

                dve.wait_ge(consts, 5)
                center(0, 0)
                normalise(0, 0)
                dve.wait_ge(params_in, 16 * 9)
                image(0, 0, False)
                image(1, 1, False)
                with dve.Fori(1, B // 2 - 1) as it:
                    image(2 * it, 0, False)
                    image(2 * it + 1, 1, False)
                image(B - 2, 0, False)
                image(B - 1, 1, True)

            @block.scalar
            def _(act):
                def square(b):
                    act.wait_ge(centered, b + 1)
                    if not (isinstance(b, int) and b == 0):
                        act.wait_ge(var_ready, b)
                    act.activation(sq[:], xc[:], ACT.Square).then_inc(squared, 1)

                def stdev_tokens(b):
                    act.wait_ge(var_ready, b + 1)
                    act.activation(stdev[:], ps_ln[:].rearrange("p a b -> p (a b)"), ACT.Sqrt, bias=eps[:]
                                   ).then_inc(stdev_ready, 1)

                def stdev_image(b, p):
                    act.wait_ge(v_ready, 3 * b + p + 1)
                    act.activation(y_std[:, p:p + 1], ps_tiny[:, 4 + p:5 + p], ACT.Sqrt, bias=eps[:]
                                   ).then_inc(y_std_ready, 1)

                def gelu(b, p):
                    act.wait_ge(affine_ready, 3 * b + p + 1)
                    for ct in range(CT):
                        op = act.activation(y[p][:, ct, :], y[p][:, ct, :], ACT.Gelu, bias=a_bias[:, p, ct:ct + 1],
                                            scale=a_scale[:, p, ct:ct + 1])
                    if p:
                        op.then_inc(gelu_done, 1)
                    else:
                        op.then_inc(scaled_from, 1)
                        act.wait_ge(scaled_from, b + 1)
                        act.activation(y[0][:], y[0][:], ACT.Copy, scale=SCALE).then_inc(q_done, 1)

                def image(b, last):
                    for g in range(GROUPS):
                        p, ct, half = g // 4, g // 2 % 2, g % 2
                        if g % 4 == 0 and not (isinstance(b, int) and b == 0):
                            act.wait_ge(stored[p], 16 * b)
                        act.wait_ge(conv_done, GROUPS * b + g + 1)
                        out = y[p][:, ct, half * HALF:(half + 1) * HALF] if p == 0 else y[p][:, ct, ::-1][
                            :, half * HALF:(half + 1) * HALF]
                        act.activation(out, ps_conv[g % 4][:], ACT.Copy).then_inc(conv_copied, 1)
                        if g == 4 and not last:
                            square(b + 1)
                        if g == 7 and not last:
                            stdev_tokens(b + 1)
                        if g in (5, 9):
                            stdev_image(b, p - 1)
                        if g == 6 or g == 10:
                            act.wait_ge(conv_copied, GROUPS * b + g + 1)
                            gelu(b, p - 1)
                    stdev_image(b, 2)
                    act.wait_ge(conv_copied, GROUPS * b + GROUPS)
                    gelu(b, 2)

                act.wait_ge(consts, 5)
                square(0)
                stdev_tokens(0)
                image(0, False)
                image(1, False)
                with act.Fori(1, B // 2 - 1) as it:
                    image(2 * it, False)
                    image(2 * it + 1, False)
                image(B - 2, False)
                image(B - 1, True)


def attend(nc, qkv, table, attended):
    TILES = N // P
    ROWS = P // IW
    U = IH + ROWS * (TILES - 1)
    KT = N // P
    QUART = KT // 2
    with ExitStack() as ctx:
        s = Space(nc, ctx, "attend")
        bias = s.sb("bias", [P, U * IW])
        q = [s.sb(f"q{j}", [DH, N]) for j in range(2)]
        k = [s.sb(f"k{j}", [DH, N]) for j in range(2)]
        v = [s.sb(f"v{j}", [DH, N]) for j in range(2)]
        vt = [s.sb(f"vt{j}", [P, KT, 2 * DH]) for j in range(2)]
        neg = [s.sb(f"neg{j}", [P, N]) for j in range(2)]
        low = [s.sb(f"low{j}", [P, 1]) for j in range(2)]
        prob = [s.sb(f"prob{j}", [P, N]) for j in range(2)]
        pt = [s.sb(f"pt{j}", [P, KT, HALF]) for j in range(2)]
        recip = s.sb("recip", [DH, HALF])
        out = [s.sb(f"out{j}", [DH, HALF]) for j in range(2)]
        ident = s.sb("ident", [P, P])
        ps_s = [s.ps(f"ps_s{j}", [P, 2, HALF]) for j in range(2)]
        ps_t = [s.ps(f"ps_t{j}", [P, QUART, P]) for j in range(2)]
        ps_o = s.ps("ps_o", [2 * DH, HALF])
        ps_v = s.ps("ps_v", [P, KT, DH])

        consts, ident_zero = s.sem("consts"), s.sem("ident_zero")
        loaded = [s.sem(f"loaded{j}") for j in range(2)]
        bias_loaded = s.sem("bias_loaded")
        s_ready = s.sem("s_ready")
        t_ready = [s.sem(f"t_ready{j}") for j in range(2)]
        v_ready, recip_done = s.sem("v_ready"), s.sem("recip_done")
        stored = [s.sem(f"stored{j}") for j in range(2)]
        neg_count, exp_count = s.sem("neg_count"), s.sem("exp_count")
        pv_count, out_count = s.sem("pv_count"), s.sem("out_count")
        vt_count, waited = s.sem("vt_count"), s.sem("waited")
        ev_count = [s.sem(f"ev_count{j}") for j in range(2)]
        CREDIT_NEG = CREDIT_EXP = CREDIT_T = 2
        CREDIT_S = 2 * TILES
        CREDIT_PV = 3
        CREDIT_OUT = CREDIT_VT = CREDIT_EV = 1

        with nc.Block() as block:

            @block.sync
            def _(sp):
                for j in range(2):
                    sp.sem_inc(stored[j], 16)

                def head(h):
                    sp.wait_ge(neg_count, B * TILES * h + CREDIT_NEG)
                    for yl in range(ROWS):
                        src = bass.AP(table.tensor, h * (2 * IH - 1) * (2 * IW - 1) + yl * (2 * IW - 1),
                                      [[1, IW], [2 * IW - 1, U], [1, IW]])
                        sp.dma_start(bias[yl * IW:(yl + 1) * IW, :], src).then_inc(bias_loaded, 16)

                def unit(u, j, h, b):
                    sp.wait_ge(s_ready, TILES * (u + 1))
                    for p, dst in enumerate((q, k, v)):
                        sp.dma_start(dst[j][:], qkv[p, bass.ds(b, 1), bass.ds(h * DH, DH)].rearrange("a p n -> (a p) n")
                                     ).then_inc(loaded[j], 16)

                with sp.Fori(0, HEADS) as h:
                    head(h)
                    with sp.Fori(0, B // 2) as bp:
                        for j in range(2):
                            unit(B * h + 2 * bp + j, j, h, 2 * bp + j)
                for j in range(2):
                    sp.wait_ge(stored[j], 16 * HEADS * B + 16)

            @block.gpsimd
            def _(pool):
                pool.memset(ident[:], 0.0).then_inc(ident_zero, 1)
                pool.wait_ge(ident_zero, 1)
                pool.affine_select(out=ident[:], in_=ident[:], compare_op=ALU.not_equal, fill=1.0, base=0,
                                   pattern=[[-1, P]], channel_multiplier=1).then_inc(consts, 1)
                for j in range(2):
                    pool.memset(vt[j][:], 1.0).then_inc(consts, 1)

            @block.tensor
            def _(pe):
                pe.sem_inc(s_ready, CREDIT_S)
                pe.sem_inc(t_ready[1], CREDIT_T)
                pe.sem_inc(pv_count, CREDIT_PV)

                def values(u, j):
                    pe.wait_ge(loaded[j], 24 * (u - j) + 48)
                    pe.wait_ge(vt_count, u + CREDIT_VT)
                    pe.sem_inc(waited, 1)
                    for kt in range(KT):
                        mm = pe.transpose(ps_v[:, kt, :], v[j][:, kt * P:(kt + 1) * P], ident[0:DH, 0:DH])
                    mm.then_inc(v_ready, 1)

                def scores(g, u, j, t):
                    pe.wait_ge(neg_count, g + 1)
                    for half in range(2):
                        mm = pe.matmul(ps_s[t % 2][:, half, :], q[j][:, t * P:(t + 1) * P],
                                       k[j][:, half * HALF:(half + 1) * HALF], start=True, stop=True)
                    mm.then_inc(s_ready, 1)

                def turn(g, t):
                    pe.wait_ge(exp_count, g + 1 + CREDIT_EXP)
                    for bank in range(2):
                        pe.wait_ge(ev_count[bank], g + CREDIT_EV)
                        for i in range(QUART):
                            kt = bank * QUART + i
                            mm = pe.transpose(ps_t[bank][:, i, :], prob[t % 2][:, kt * P:(kt + 1) * P], ident[:])
                        mm.then_inc(t_ready[bank], 1)

                def weigh(hg, u, j, half):
                    for bank in range(2):
                        pe.wait_ge(ev_count[bank], 4 * hg + 4 + CREDIT_EV)
                    pe.wait_ge(vt_count, u + 1 + CREDIT_VT)
                    pe.wait_ge(out_count, hg + CREDIT_OUT)
                    for kt in range(KT):
                        mm = pe.matmul(ps_o[:], vt[j][:, kt, :], pt[half][:, kt, :], start=kt == 0, stop=kt == KT - 1)
                    mm.then_inc(pv_count, 1)

                pe.wait_ge(consts, 3)
                with pe.Fori(0, HEADS) as h:
                    with pe.Fori(0, B // 2) as bp:
                        u0 = B * h + 2 * bp
                        g0 = TILES * u0
                        values(u0, 0)
                        scores(g0, u0, 0, 0)
                        for n in range(2 * TILES):
                            j, t = n // TILES, n % TILES
                            if n + 1 < 2 * TILES:
                                if t == TILES - 1:
                                    values(u0 + 1, 1)
                                scores(g0 + n + 1, u0 + (n + 1) // TILES, (n + 1) // TILES, (n + 1) % TILES)
                            turn(g0 + n, t)
                            if n % 4 == 0 and n:
                                weigh(2 * u0 + n // 4 - 1, u0 + (n - 1) // TILES, (n - 1) // TILES, (n // 4 - 1) % 2)
                        weigh(2 * u0 + 3, u0 + 1, 1, 1)

            @block.vector
            def _(dve):
                dve.sem_inc(neg_count, CREDIT_NEG)
                dve.sem_inc(ev_count[0], CREDIT_EV)
                dve.sem_inc(vt_count, CREDIT_VT)
                dve.sem_inc(out_count, CREDIT_OUT)

                def values(u, j):
                    dve.wait_ge(v_ready, u + 1)
                    dve.wait_ge(pv_count, 2 * u + 1)
                    dve.tensor_copy(vt[j][:, :, 0:DH], ps_v[:]).then_inc(vt_count, 1)

                def negate(g, h, t):
                    dve.wait_ge(bias_loaded, 16 * ROWS * (h + 1))
                    dve.wait_ge(s_ready, g + 1 + CREDIT_S)
                    dve.wait_ge(exp_count, g + 1)
                    dve.sem_inc(waited, 1)
                    dve.tensor_tensor_reduce(neg[t % 2][:], ps_s[t % 2][:].rearrange("p a b -> p (a b)"),
                                             bias[:, t * P:t * P + N], -1.0, BIG, ALU.add, ALU.min, low[t % 2][:]
                                             ).then_inc(neg_count, 1)

                def keep(g, hg, t):
                    dve.wait_ge(t_ready[0], g + 1)
                    dve.wait_ge(pv_count, hg + 2)
                    dve.tensor_copy(pt[t // 4][:, 0:QUART, t % 4 * P:(t % 4 + 1) * P], ps_t[0][:]
                                    ).then_inc(ev_count[0], 1)

                def finish(hg, u, half):
                    dve.wait_ge(pv_count, hg + 1 + CREDIT_PV)
                    dve.reciprocal(recip[:], ps_o[DH:2 * DH, :]).then_inc(recip_done, 1)
                    dve.wait_ge(recip_done, hg + 1)
                    dve.wait_ge(stored[half], 16 * u + 16)
                    dve.tensor_tensor(out[half][:], ps_o[0:DH, :], recip[:], ALU.mult).then_inc(out_count, 1)

                dve.wait_ge(consts, 3)
                with dve.Fori(0, HEADS) as h:
                    with dve.Fori(0, B // 2) as bp:
                        u0 = B * h + 2 * bp
                        g0 = TILES * u0
                        values(u0, 0)
                        negate(g0, h, 0)
                        for n in range(2 * TILES):
                            t = n % TILES
                            if n + 1 < 2 * TILES:
                                if t == TILES - 1:
                                    values(u0 + 1, 1)
                                negate(g0 + n + 1, h, (n + 1) % TILES)
                            keep(g0 + n, 2 * u0 + n // 4, t)
                            if n % 4 == 1 and n > 1:
                                finish(2 * u0 + n // 4 - 1, u0 + (n - 2) // TILES, (n // 4 - 1) % 2)
                        finish(2 * u0 + 3, u0 + 1, 1)

            @block.scalar
            def _(act):
                act.sem_inc(exp_count, CREDIT_EXP)
                act.sem_inc(ev_count[1], CREDIT_EV)

                def exps(g, t):
                    act.wait_ge(neg_count, g + 1 + CREDIT_NEG)
                    act.wait_ge(t_ready[1], g + 1)
                    act.activation(prob[t % 2][:], neg[t % 2][:], ACT.Exp, bias=low[t % 2][:], scale=-1.0
                                   ).then_inc(exp_count, 1)

                def keep(g, hg, t):
                    act.wait_ge(t_ready[1], g + 1 + CREDIT_T)
                    act.wait_ge(pv_count, hg + 2)
                    act.activation(pt[t // 4][:, QUART:KT, t % 4 * P:(t % 4 + 1) * P], ps_t[1][:], ACT.Copy
                                   ).then_inc(ev_count[1], 1)

                def store(hg, h, b, half):
                    act.wait_ge(out_count, hg + 1 + CREDIT_OUT)
                    act.dma_start(attended[bass.ds(b, 1), bass.ds(h * DH, DH), half * HALF:(half + 1) * HALF
                                           ].rearrange("a p n -> (a p) n"), out[half][:]).then_inc(stored[half], 16)

                with act.Fori(0, HEADS) as h:
                    with act.Fori(0, B // 2) as bp:
                        u0 = B * h + 2 * bp
                        g0 = TILES * u0
                        exps(g0, 0)
                        for n in range(2 * TILES):
                            if n + 1 < 2 * TILES:
                                exps(g0 + n + 1, (n + 1) % TILES)
                            keep(g0 + n, 2 * u0 + n // 4, n % TILES)
                            if n % 4 == 2 and n > 2:
                                m = n // 4 - 1
                                store(2 * u0 + m, h, 2 * bp + m // 2, m % 2)
                        store(2 * u0 + 3, h, 2 * bp + 1, 1)


def mix(nc, attended, x, w_out, b_out, w_gat, x_mid, tokens, features):
    EPS = 1e-5
    KT = HALF // P
    NF = w_gat.shape[1]
    with ExitStack() as ctx:
        s = Space(nc, ctx, "mix")
        wo = s.sb("wo", [P, CT, C])
        wg = s.sb("wg", [P, CT, NF])
        bo = s.sb("bo", [P, CT])
        ones_c = s.sb("ones_c", [P, P])
        eps = s.sb("eps", [P, 1])
        att = [s.sb(f"att{i}", [P, CT, HALF]) for i in range(2)]
        xin = [s.sb(f"xin{i}", [P, CT, HALF]) for i in range(2)]
        mid = [s.sb(f"mid{i}", [P, CT, HALF]) for i in range(2)]
        cen = [s.sb(f"cen{i}", [P, CT, HALF]) for i in range(2)]
        sq = [s.sb(f"sq{i}", [P, CT, HALF]) for i in range(2)]
        stdev = [s.sb(f"stdev{i}", [P, HALF]) for i in range(2)]
        rstd = [s.sb(f"rstd{i}", [P, HALF]) for i in range(2)]
        tok = [s.sb(f"tok{i}", [P, CT, HALF]) for i in range(2)]
        ps_x = [s.ps(f"ps_x{i}", [P, CT, HALF]) for i in range(2)]
        ps_m = [s.ps(f"ps_m{i}", [P, HALF]) for i in range(2)]
        ps_h = [s.ps(f"ps_h{i}", [P, KT, NF]) for i in range(2)]
        params_in, consts, began = s.sem("params_in"), s.sem("consts"), s.sem("began")
        names = ("loaded", "projected", "summed", "mean_ready", "centered", "squared", "var_ready", "stdev_ready",
                 "rstd_ready", "tok_ready", "h_ready", "h_kept", "mid_stored", "tok_stored")
        (loaded, projected, summed, mean_ready, centered, squared, var_ready, stdev_ready, rstd_ready, tok_ready,
         h_ready, h_kept, mid_stored, tok_stored) = ([s.sem(f"{n}{i}") for i in range(2)] for n in names)

        with nc.Block() as block:

            @block.sync
            def _(sp):
                sp.dma_start(wo[:], w_out.rearrange("(c p) o -> p c o", p=P)).then_inc(params_in, 16)
                sp.dma_start(wg[:], w_gat.rearrange("(c p) o -> p c o", p=P)).then_inc(params_in, 16)
                sp.dma_start(bo[:], b_out).then_inc(params_in, 16)
                for i in range(2):
                    sp.sem_inc(summed[i], 1)
                with sp.Fori(0, B) as b:
                    for i in range(2):
                        sp.wait_ge(summed[i], b + 1)
                        for src, dst in ((attended, att), (x, xin)):
                            sp.dma_start(dst[i][:], src[bass.ds(b, 1), :, i * HALF:(i + 1) * HALF].rearrange(
                                "a (c p) n -> p (a c) n", p=P)).then_inc(loaded[i], 16)
                for i in range(2):
                    sp.wait_ge(mid_stored[i], 16 * B + 16)
                    sp.wait_ge(tok_stored[i], 16 * B + 16)

            @block.tensor
            def _(pe):
                pe.wait_ge(params_in, 48)
                pe.wait_ge(consts, 2)
                with pe.Fori(0, B) as b:
                    for i in range(2):
                        pe.wait_ge(loaded[i], 32 * b + 32)
                        pe.wait_ge(summed[i], b + 1)
                        for o in range(CT):
                            for c in range(CT):
                                mm = pe.matmul(ps_x[i][:, o, :], wo[:, c, o * P:(o + 1) * P], att[i][:, c, :],
                                               start=c == 0, stop=c == CT - 1)
                        mm.then_inc(projected[i], 1)
                    for i in range(2):
                        pe.wait_ge(summed[i], b + 2)
                        pe.wait_ge(stdev_ready[i], b + 1)
                        for c in range(CT):
                            mm = pe.matmul(ps_m[i][:], ones_c[:], mid[i][:, c, :], start=c == 0, stop=c == CT - 1)
                        mm.then_inc(mean_ready[i], 1)
                    for i in range(2):
                        pe.wait_ge(squared[i], b + 1)
                        for c in range(CT):
                            mm = pe.matmul(ps_m[i][:], ones_c[:], sq[i][:, c, :], start=c == 0, stop=c == CT - 1)
                        mm.then_inc(var_ready[i], 1)
                    for i in range(2):
                        pe.wait_ge(tok_ready[i], b + 1)
                        pe.wait_ge(h_kept[i], b + 1)
                        for t in range(KT):
                            for c in range(CT):
                                mm = pe.matmul(ps_h[i][:, t, :], tok[i][:, c, t * P:(t + 1) * P], wg[:, c, :],
                                               start=c == 0, stop=c == CT - 1)
                        mm.then_inc(h_ready[i], 1)

            @block.vector
            def _(dve):
                dve.memset(ones_c[:], 1.0 / C).then_inc(consts, 1)
                dve.memset(eps[:], EPS).then_inc(consts, 1)
                for i in range(2):
                    dve.sem_inc(h_kept[i], 1)
                dve.wait_ge(params_in, 48)
                with dve.Fori(0, B) as b:
                    for i in range(2):
                        dve.wait_ge(projected[i], b + 1)
                        dve.wait_ge(mid_stored[i], 16 * b + 16)
                        for o in range(CT):
                            op = dve.scalar_tensor_tensor(mid[i][:, o, :], ps_x[i][:, o, :], bo[:, o:o + 1],
                                                          xin[i][:, o, :], ALU.add, ALU.add)
                        op.then_inc(summed[i], 1)
                    for i in range(2):
                        dve.wait_ge(mean_ready[i], b + 1)
                        for c in range(CT):
                            op = dve.tensor_tensor(cen[i][:, c, :], mid[i][:, c, :], ps_m[i][:], ALU.subtract)
                        op.then_inc(centered[i], 1)
                    for i in range(2):
                        dve.wait_ge(stdev_ready[i], b + 2)
                        dve.reciprocal(rstd[i][:], stdev[i][:]).then_inc(rstd_ready[i], 1)
                        dve.wait_ge(rstd_ready[i], b + 1)
                        dve.wait_ge(tok_stored[i], 16 * b + 16)
                        for c in range(CT):
                            op = dve.tensor_tensor(tok[i][:, c, :], cen[i][:, c, :], rstd[i][:], ALU.mult)
                        op.then_inc(tok_ready[i], 1)
                    for i in range(2):
                        dve.wait_ge(h_ready[i], b + 1)
                        dve.tensor_copy(features[:, bass.ds(b * 2 * KT + i * KT, KT), :], ps_h[i][:]
                                        ).then_inc(h_kept[i], 1)

            @block.scalar
            def _(act):
                for i in range(2):
                    act.sem_inc(mid_stored[i], 16)
                    act.sem_inc(tok_stored[i], 16)
                    act.sem_inc(stdev_ready[i], 1)
                act.wait_ge(consts, 2)
                with act.Fori(0, B) as b:
                    for i in range(2):
                        act.wait_ge(summed[i], b + 2)
                        act.dma_start(x_mid[bass.ds(b, 1), :, i * HALF:(i + 1) * HALF].rearrange(
                            "a (c p) n -> p (a c) n", p=P), mid[i][:]).then_inc(mid_stored[i], 16)
                    for i in range(2):
                        act.wait_ge(centered[i], b + 1)
                        act.activation(sq[i][:], cen[i][:], ACT.Square).then_inc(squared[i], 1)
                    for i in range(2):
                        act.wait_ge(var_ready[i], b + 1)
                        act.activation(stdev[i][:], ps_m[i][:], ACT.Sqrt, bias=eps[:]).then_inc(stdev_ready[i], 1)
                    for i in range(2):
                        act.wait_ge(tok_ready[i], b + 1)
                        act.dma_start(tokens[bass.ds(b, 1), :, i * HALF:(i + 1) * HALF].rearrange(
                            "a (c p) n -> p (a c) n", p=P), tok[i][:]).then_inc(tok_stored[i], 16)


def experts(nc, tokens, x_mid, gates, w1, b1, w2, b2, out):
    E, _, F = w1.shape
    FT = F // P
    with ExitStack() as ctx:
        s = Space(nc, ctx, "experts")
        w1s = s.sb("w1", [P, E, CT, F])
        w2s = s.sb("w2", [P, E, FT, C])
        b1s = s.sb("b1", [P, E, FT])
        b2s = s.sb("b2", [E, C])
        pick = s.sb("pick", [E, E, P])
        pick0 = s.sb("pick0", [E, E, P])
        tok = [s.sb(f"tok{i}", [P, CT, HALF]) for i in range(2)]
        mid = [s.sb(f"mid{i}", [P, CT, HALF]) for i in range(2)]
        gate = [s.sb(f"gate{i}", [E, HALF]) for i in range(2)]
        gate_all = [s.sb(f"gate_all{j}", [P, HALF]) for j in range(2)]
        hid = [s.sb(f"hid{j}", [P, FT, HALF]) for j in range(2)]
        res = [s.sb(f"res{i}", [P, CT, HALF]) for i in range(2)]
        ps_h = [s.ps(f"ps_h{t}", [P, HALF]) for t in range(FT)]
        ps_g = s.ps("ps_g", [P, HALF])
        ps_y = s.ps("ps_y", [P, CT, HALF])
        params_in, consts, picked = s.sem("params_in"), s.sem("consts"), s.sem("picked")
        loaded = [s.sem(f"loaded{i}") for i in range(2)]
        stored = [s.sem(f"stored{i}") for i in range(2)]
        g_ready, g_kept = s.sem("g_ready"), s.sem("g_kept")
        h_ready, h_gelu, h_gated = s.sem("h_ready"), s.sem("h_gelu"), s.sem("h_gated")
        y_part, y_ready, y_done = s.sem("y_part"), s.sem("y_ready"), s.sem("y_done")

        with nc.Block() as block:

            @block.sync
            def _(sp):
                sp.dma_start(w1s[:], w1.rearrange("e (c p) f -> p e c f", p=P)).then_inc(params_in, 16)
                sp.dma_start(w2s[:], w2.rearrange("e (t p) o -> p e t o", p=P)).then_inc(params_in, 16)
                sp.dma_start(b1s[:], b1).then_inc(params_in, 16)
                sp.dma_start(b2s[:], b2).then_inc(params_in, 16)
                sp.sem_inc(y_done, 2)
                with sp.Fori(0, B) as b:
                    for i in range(2):
                        sp.wait_ge(y_done, 2 * b + i + 1)
                        cols = slice(i * HALF, (i + 1) * HALF)
                        for src, dst in ((tokens, tok), (x_mid, mid)):
                            sp.dma_start(dst[i][:], src[bass.ds(b, 1), :, cols].rearrange(
                                "a (c p) n -> p (a c) n", p=P)).then_inc(loaded[i], 16)
                        sp.dma_start(gate[i][:], gates[:, bass.ds(b, 1), cols].rearrange("e a n -> e (a n)")
                                     ).then_inc(loaded[i], 16)
                for i in range(2):
                    sp.wait_ge(stored[i], 16 * B + 16)

            @block.gpsimd
            def _(pool):
                pool.memset(pick0[:], 1.0).then_inc(picked, 1)
                pool.wait_ge(picked, 1)
                pool.affine_select(out=pick[:], in_=pick0[:], compare_op=ALU.is_equal, fill=0.0, base=0,
                                   pattern=[[-1, E], [0, P]], channel_multiplier=1).then_inc(consts, 1)

            @block.tensor
            def _(pe):
                def hidden(n, e, i):
                    pe.wait_ge(g_kept, n + 1)
                    pe.matmul(ps_g[:], pick[:, e, :], gate[i][:], start=True, stop=True).then_inc(g_ready, 1)
                    for t in range(FT):
                        pe.wait_ge(h_gelu, FT * n + t + 1)
                        for c in range(CT):
                            mm = pe.matmul(ps_h[t][:], w1s[:, e, c, t * P:(t + 1) * P], tok[i][:, c, :],
                                           start=c == 0, stop=c == CT - 1)
                        mm.then_inc(h_ready, 1)

                def output(n, e, i):
                    for t in range(FT):
                        pe.wait_ge(h_gated, FT * n + t + 1)
                        for o in range(CT):
                            mm = pe.matmul(ps_y[:, o, :], w2s[:, e, t, o * P:(o + 1) * P], hid[e % 2][:, t, :],
                                           start=False, stop=False, skip_group_check=True)
                    mm.then_inc(y_part, 1)

                pe.wait_ge(params_in, 64)
                pe.wait_ge(consts, 1)
                pe.sem_inc(y_part, 2)
                with pe.Fori(0, B) as b:
                    for i in range(2):
                        c0 = 2 * b + i
                        pe.wait_ge(loaded[i], 48 * b + 48)
                        hidden(E * c0, 0, i)
                        pe.wait_ge(y_done, c0 + 2)
                        for o in range(CT):
                            pe.matmul(ps_y[:, o, :], b2s[:, o * P:(o + 1) * P], gate[i][:], start=True, stop=False,
                                      skip_group_check=True)
                        for e in range(E):
                            if e + 1 < E:
                                hidden(E * c0 + e + 1, e + 1, i)
                            output(E * c0 + e, e, i)

            @block.scalar
            def _(act):
                act.sem_inc(h_gelu, FT)
                act.sem_inc(g_kept, 1)
                for i in range(2):
                    act.sem_inc(stored[i], 16)
                act.wait_ge(params_in, 64)
                with act.Fori(0, B) as b:
                    for i in range(2):
                        c0 = 2 * b + i
                        for e in range(E):
                            n = E * c0 + e
                            act.wait_ge(g_ready, n + 1)
                            act.wait_ge(y_part, n + 1)
                            act.activation(gate_all[e % 2][:], ps_g[:], ACT.Copy).then_inc(g_kept, 1)
                            for t in range(FT):
                                act.wait_ge(h_ready, FT * n + t + 1)
                                act.activation(hid[e % 2][:, t, :], ps_h[t][:], ACT.Gelu, bias=b1s[:, e, t:t + 1]
                                               ).then_inc(h_gelu, 1)
                        act.wait_ge(y_done, c0 + 3)
                        act.dma_start(out[bass.ds(b, 1), :, i * HALF:(i + 1) * HALF].rearrange(
                            "a (c p) n -> p (a c) n", p=P), res[i][:]).then_inc(stored[i], 16)

            @block.vector
            def _(dve):
                with dve.Fori(0, B) as b:
                    for i in range(2):
                        c0 = 2 * b + i
                        for e in range(E):
                            n = E * c0 + e
                            dve.wait_ge(g_kept, n + 2)
                            for t in range(FT):
                                dve.wait_ge(h_gelu, FT * n + t + 1 + FT)
                                dve.tensor_tensor(hid[e % 2][:, t, :], hid[e % 2][:, t, :], gate_all[e % 2][:],
                                                  ALU.mult).then_inc(h_gated, 1)
                        dve.wait_ge(y_part, E * c0 + E + 2)
                        dve.wait_ge(stored[i], 16 * b + 16)
                        dve.tensor_tensor(res[i][:], ps_y[:], mid[i][:], ALU.add).then_inc(y_done, 1)


HI = M // P
KEY_BASE = 0x20000000


def sort_edges(nc, edges, counts, keys):
    E = edges.shape[1]
    COLS = E // P
    CH = 256
    SUB = 32
    NODE_BITS = M.bit_length() - 1
    LO_BITS = P.bit_length() - 1
    with ExitStack() as ctx:
        s = Space(nc, ctx, "sort")
        src = [s.sb(f"src{i}", [P, CH], I32) for i in range(2)]
        dst = [s.sb(f"dst{i}", [P, CH], I32) for i in range(2)]
        hi_i, lo_i, key_i = (s.sb(n, [P, CH], I32) for n in ("hi_i", "lo_i", "key_i"))
        m_src, m_dst, m_both, pen = (s.sb(n, [P, CH], I32) for n in ("m_src", "m_dst", "m_both", "pen"))
        hi = s.sb("hi", [P, CH], BF16)
        lo = s.sb("lo", [P, CH], BF16)
        ramp_i = s.sb("ramp_i", [P, P], I32)
        ramp = s.sb("ramp", [P, P, SUB], BF16)
        hot_hi = [s.sb(f"hot_hi{i}", [P, HI, SUB], BF16) for i in range(2)]
        hot_lo = [s.sb(f"hot_lo{i}", [P, P, SUB], BF16) for i in range(2)]
        zero = s.sb("zero", [P, P], BF16)
        ps = s.ps("ps", [P, HI])
        loaded = [s.sem(f"loaded{i}") for i in range(2)]
        ramped, consts, split, split2, parsed = (s.sem(n) for n in ("ramped", "consts", "split", "split2", "parsed"))
        hot, counted, all_counted, kept = s.sem("hot"), s.sem("counted"), s.sem("all_counted"), s.sem("kept")
        BLOCKS = CH // SUB
        NCH = COLS // CH

        with nc.Block() as block:

            @block.sync
            def _(sp):
                sp.sem_inc(parsed, 2)
                with sp.Fori(0, NCH // 2) as n:
                    for i in range(2):
                        sp.wait_ge(parsed, 2 * n + i + 1)
                        for row, buf in ((0, src), (1, dst)):
                            sp.dma_start(buf[i][:], edges[row].rearrange("(p j) -> p j", p=P)[
                                :, bass.ds(2 * CH * n + i * CH, CH)]).then_inc(loaded[i], 16)

            @block.gpsimd
            def _(pool):
                pool.iota(ramp_i[:], [[1, P]], base=0, channel_multiplier=0).then_inc(ramped, 1)

            @block.vector
            def _(dve):
                dve.memset(zero[:], 0.0).then_inc(consts, 1)
                dve.wait_ge(ramped, 1)
                dve.tensor_copy(ramp[:], ramp_i[:].unsqueeze(2).to_broadcast([P, P, SUB])).then_inc(consts, 1)
                dve.sem_inc(counted, 2)
                dve.wait_ge(consts, 2)
                with dve.Fori(0, NCH // 2) as n:
                    for i in range(2):
                        c = 2 * n + i
                        dve.wait_ge(loaded[i], 32 * n + 32)
                        dve.tensor_scalar(hi_i[:], dst[i][:], LO_BITS, None, ALU.logical_shift_right).then_inc(split, 1)
                        dve.tensor_scalar(lo_i[:], dst[i][:], P - 1, None, ALU.bitwise_and).then_inc(split, 1)
                        dve.tensor_scalar(m_src[:], src[i][:], float(M - 1), -1.0, ALU.is_lt, ALU.mult).then_inc(split, 1)
                        dve.tensor_scalar(m_dst[:], dst[i][:], float(M), -1.0, ALU.is_lt, ALU.mult).then_inc(split, 1)
                        dve.tensor_scalar(pen[:], src[i][:], float(M - 1), float(HI), ALU.is_lt, ALU.mult).then_inc(split, 1)
                        dve.tensor_scalar(key_i[:], src[i][:], NODE_BITS, KEY_BASE, ALU.logical_shift_left,
                                          ALU.bitwise_or).then_inc(split, 1)
                        dve.wait_ge(split, 6 * c + 6)
                        dve.tensor_tensor(m_both[:], m_src[:], m_dst[:], ALU.bitwise_and).then_inc(split2, 1)
                        dve.tensor_tensor(key_i[:], key_i[:], dst[i][:], ALU.bitwise_or).then_inc(split2, 1)
                        dve.tensor_tensor(hi[:], hi_i[:], pen[:], ALU.add).then_inc(split2, 1)
                        dve.tensor_copy(lo[:], lo_i[:]).then_inc(split2, 1)
                        dve.wait_ge(split2, 4 * c + 4)
                        dve.tensor_tensor(keys[:].bitcast(I32)[:, bass.ds(c * CH, CH)], key_i[:], m_both[:], ALU.bitwise_and
                                          ).then_inc(parsed, 1)
                        for b in range(BLOCKS):
                            cols = slice(b * SUB, (b + 1) * SUB)
                            dve.wait_ge(counted, BLOCKS * c + b + 1)
                            dve.tensor_tensor(hot_hi[b % 2][:], ramp[:, 0:HI, :],
                                              hi[:, cols].unsqueeze(1).to_broadcast([P, HI, SUB]), ALU.is_equal)
                            dve.tensor_tensor(hot_lo[b % 2][:], ramp[:],
                                              lo[:, cols].unsqueeze(1).to_broadcast([P, P, SUB]), ALU.is_equal
                                              ).then_inc(hot, 1)
                dve.wait_ge(all_counted, 1)
                dve.tensor_copy(counts[:], ps[:]).then_inc(kept, 1)
                dve.wait_ge(kept, 1)

            @block.tensor
            def _(pe):
                pe.wait_ge(consts, 2)
                pe.matmul(ps[:], zero[:], zero[:, 0:HI], start=True, stop=False, skip_group_check=True)
                with pe.Fori(0, NCH // 2) as n:
                    for i in range(2):
                        for b in range(BLOCKS):
                            pe.wait_ge(hot, BLOCKS * (2 * n + i) + b + 1)
                            for c in range(SUB):
                                mm = pe.matmul(ps[:], hot_lo[b % 2][:, :, c], hot_hi[b % 2][:, :, c],
                                               start=False, stop=False, skip_group_check=True)
                            mm.then_inc(counted, 1)
                pe.matmul(ps[:], zero[:], zero[:, 0:HI], start=False, stop=True, skip_group_check=True
                          ).then_inc(all_counted, 1)


class Steps:

    def __init__(self, eng, sem, base=0):
        self.eng, self.sem, self.n = eng, sem, base

    def done(self, op):
        self.n = self.n + 1
        return op.then_inc(self.sem, 1)

    def wait(self):
        self.eng.wait_ge(self.sem, self.n)


def route(nc, features, counts, keys, att_src, att_dst, b_gat, gamma, beta, node_rows, state_rows, gates):
    H, E = att_src.shape[1], att_src.shape[2]
    HE = H * E
    NROW = H + HE
    SROW = 3 * H + HE
    MX, DEN, ACC = H, 2 * H, 3 * H
    SLOPE = 0.2
    EPS = 1e-5
    NODE_BITS = M.bit_length() - 1
    COLS = keys.shape[1]
    with ExitStack() as ctx:
        s = Space(nc, ctx, "route")
        a_s, a_d = s.sb("a_s", [P, HE]), s.sb("a_d", [P, HE])
        vec = s.sb("vec", [P, 3, HE])
        prod = s.sb("prod", [P, HI, HE])
        node = s.sb("node", [P, HI, NROW])
        state = s.sb("state", [P, HI, SROW])
        last = s.sb("last", [P, NROW])
        has = s.sb("has", [P, HI])
        has_neg = s.sb("has_neg", [P, HI])
        cand = s.sb("cand", [P, HI, H])
        raw = s.sb("raw", [P, 3, HI, H])
        act3 = s.sb("act3", [P, 3, HI, H])
        wts = s.sb("wts", [P, 2, HI, H])
        part = s.sb("part", [P, HI, HE])
        some = s.sb("some", [P, COLS], BF16)
        num = s.sb("num", [P, 1])
        num_all = s.sb("num_all", [P, 1])
        num_i = s.sb("num_i", [P, 1], I32)
        rounds = s.sb("rounds", [P, 1], I32)
        spare_i = s.sb("spare_i", [P, 1], I32)
        spare = s.sb("spare", [P, 1])
        ident0, ident = s.sb("ident0", [P, P]), s.sb("ident", [P, P])
        ones = s.sb("ones", [P, P])
        before = s.sb("before", [P, P])
        key8 = s.sb("key8", [P, 8])
        none8, spare8, tgt_f = s.sb("none8", [P, 8]), s.sb("spare8", [P, 8]), s.sb("tgt_f", [P, 8])
        tgt0_i, src_i, tgt_i, put_i = (s.sb(n, [P, 8], I32) for n in ("tgt0_i", "src_i", "tgt_i", "put_i"))
        src_row = s.sb("src_row", [P, 8, NROW])
        same = [s.sb(f"same{j}", [P, P]) for j in range(2)]
        differ = s.sb("differ", [P, P])
        scratch = s.sb("scratch", [P, P])
        mates = s.sb("mates", [P, 1])
        away, step_f, put_f = s.sb("away", [P, 1]), s.sb("step_f", [P, 1]), s.sb("put_f", [P, 1])
        masked = s.sb("masked", [P, H, P])
        best = [s.sb(f"best{j}", [P, H]) for j in range(2)]
        row = s.sb("row", [P, SROW])
        new = s.sb("new", [P, SROW])
        z, zl, d = s.sb("z", [P, 3, H]), s.sb("zl", [P, 3, H]), s.sb("d", [P, 2, H])
        load = s.sb("load", [P, H + HE])
        fade = s.sb("fade", [P, H])
        kept = s.sb("kept", [P, H + HE])
        agg = s.sb("agg", [P, HI, HE])
        g1, g2 = s.sb("g1", [P, HI, H]), s.sb("g2", [P, HI, H])
        t1, t2 = s.sb("t1", [P, HI]), s.sb("t2", [P, HI])
        eps = s.sb("eps", [P, 1])
        score, rank, cmp = s.sb("score", [P, HI, E]), s.sb("rank", [P, HI, E]), s.sb("cmp", [P, HI, E])
        gate = s.sb("gate", [P, HI, E])
        gate_t = s.sb("gate_t", [E, M])
        ps_same = s.ps("ps_same", [P, P])
        ps_best = s.ps("ps_best", [P, H, P])
        ps_sum = s.ps("ps_sum", [P, H + HE])
        ps_gate = [s.ps(f"ps_gate{j}", [E, 4 * P]) for j in range(2)]

        params_in, consts, seeded = s.sem("params_in"), s.sem("consts"), s.sem("seeded")
        node_ready, node_out, last_in = s.sem("node_ready"), s.sem("node_out"), s.sem("last_in")
        args_ready, exps_ready, state_ready, state_out = (
            s.sem(n) for n in ("args_ready", "exps_ready", "state_ready", "state_out"))
        num_ready, num_done, rounds_ready = s.sem("num_ready"), s.sem("num_done"), s.sem("rounds_ready")
        step, step2, step3 = s.sem("step"), s.sem("step2"), s.sem("step3")
        picked, decoded, round_done = s.sem("picked"), s.sem("decoded"), s.sem("round_done")
        src_in = [s.sem(f"src_in{i}") for i in range(8)]
        same_ready, best_ready, prepared = s.sem("same_ready"), s.sem("best_ready"), s.sem("prepared")
        row_in, d_ready, w_ready, load_ready = (s.sem(n) for n in ("row_in", "d_ready", "w_ready", "load_ready"))
        sum_ready, new_ready, row_out, waited = (s.sem(n) for n in ("sum_ready", "new_ready", "row_out", "waited"))
        state_in, gate_ready, gate_turned, gate_kept, gate_out = (
            s.sem(n) for n in ("state_in", "gate_ready", "gate_turned", "gate_kept", "gate_out"))
        g_var, g_std, g_arg, g_exp = (s.sem(n) for n in ("g_var", "g_std", "g_arg", "g_exp"))

        def hh(ap):
            return ap.unsqueeze(3).to_broadcast([P, HI, H, E])

        def he(ap):
            return ap.rearrange("p t (h e) -> p t h e", h=H)

        with nc.Block() as block:

            @block.sync
            def _(sp):
                sp.dma_start(a_s[:], att_src.rearrange("a h e -> a (h e)").to_broadcast([P, HE])).then_inc(params_in, 16)
                sp.dma_start(a_d[:], att_dst.rearrange("a h e -> a (h e)").to_broadcast([P, HE])).then_inc(params_in, 16)
                for n, v in enumerate((b_gat, gamma, beta)):
                    sp.dma_start(vec[:, n, :], v.to_broadcast([P, HE])).then_inc(params_in, 16)
                sp.wait_ge(node_ready, 3)
                sp.dma_start(node_rows.rearrange("(t p) r -> p t r", p=P), node[:]).then_inc(node_out, 16)
                sp.wait_ge(node_out, 16)
                sp.dma_start(last[:], node_rows[M - 1:M, :].to_broadcast([P, NROW])).then_inc(last_in, 16)
                sp.wait_ge(state_ready, 1)
                sp.dma_start(state_rows[0:M, :].rearrange("(t p) r -> p t r", p=P), state[:]).then_inc(state_out, 16)
                sp.dma_start(state_rows[M:M + P, :], state[:, 0, :]).then_inc(state_out, 16)
                sp.wait_ge(round_done, 1)
                sp.dma_start(state[:], state_rows[0:M, :].rearrange("(t p) r -> p t r", p=P)).then_inc(state_in, 16)
                sp.wait_ge(gate_kept, HI // 4 + 2)
                sp.dma_start(gates, gate_t[:]).then_inc(gate_out, 16)
                sp.wait_ge(gate_out, 16)

            @block.gpsimd
            def _(pool):
                pool.iota(spare_i[:], [[0, 1]], base=M, channel_multiplier=1).then_inc(seeded, 1)
                pool.memset(ident0[:], 0.0).then_inc(seeded, 1)
                pool.memset(ones[:], 1.0).then_inc(seeded, 1)
                pool.wait_ge(seeded, 3)
                pool.affine_select(out=ident[:], in_=ident0[:], compare_op=ALU.not_equal, fill=1.0, base=0,
                                   pattern=[[-1, P]], channel_multiplier=1).then_inc(consts, 1)
                pool.affine_select(out=before[:], in_=ones[:], compare_op=ALU.is_gt, fill=0.0, base=0,
                                   pattern=[[-1, P]], channel_multiplier=1).then_inc(consts, 1)
                pool.wait_ge(num_ready, 1)
                pool.partition_all_reduce(num_all[:], num[:], P, bass.bass_isa.ReduceOp.max).then_inc(num_done, 1)
                pool.wait_ge(state_out, 32)
                pool.wait_ge(rounds_ready, 1)
                n_rounds = pool.value_load(rounds[0:1, 0:1], min_val=1, max_val=COLS // 8)
                with pool.Fori(0, n_rounds) as r:
                    pool.wait_ge(decoded, r + 1)
                    pool.sem_inc(waited, 1)
                    for i in range(8):
                        pool.indirect_dma_start(src_row[:, i, :], None, node_rows,
                                                bass.IndirectOffsetOnAxis(src_i[:, i:i + 1], 0)).then_inc(src_in[i], 16)
                    for i in range(8):
                        n = 8 * r + i
                        pool.indirect_dma_start(row[:], None, state_rows,
                                                bass.IndirectOffsetOnAxis(tgt_i[:, i:i + 1], 0)).then_inc(row_in, 16)
                        pool.wait_ge(new_ready, n + 1)
                        pool.sem_inc(waited, 1)
                        pool.indirect_dma_start(state_rows, bass.IndirectOffsetOnAxis(put_i[:, i:i + 1], 0),
                                                new[:], None).then_inc(row_out, 16)
                        pool.wait_ge(row_out, 16 * n + 16)
                        pool.sem_inc(waited, 1)
                pool.sem_inc(round_done, 1)

            @block.tensor
            def _(pe):
                pe.wait_ge(consts, 2)
                pe.wait_ge(rounds_ready, 1)
                n_rounds = pe.value_load(rounds[0:1, 0:1], min_val=1, max_val=COLS // 8)

                with pe.Fori(0, n_rounds) as r:
                    pe.wait_ge(decoded, r + 1)
                    for i in range(9):
                        if i < 8:
                            n = 8 * r + i
                            pe.wait_ge(src_in[i], 16 * r + 16)
                            pe.wait_ge(prepared, n + 1)
                            pe.sem_inc(waited, 1)
                            pe.transpose(ps_same[:], tgt_f[:, i:i + 1].to_broadcast([P, P]), ident[:]
                                         ).then_inc(same_ready, 1)
                            for h in range(H):
                                mm = pe.transpose(ps_best[:, h, :], src_row[:, i, h:h + 1].to_broadcast([P, P]), ident[:])
                            mm.then_inc(best_ready, 1)
                        if i >= 1:
                            n = 8 * r + i - 1
                            pe.wait_ge(load_ready, n + 1)
                            pe.matmul(ps_sum[:], same[(i - 1) % 2][:], load[:], start=True, stop=True
                                      ).then_inc(sum_ready, 1)
                pe.wait_ge(gate_ready, 1)
                for g in range(HI // 4):
                    pe.wait_ge(gate_kept, g + 1)
                    for t in range(4):
                        mm = pe.transpose(ps_gate[g % 2][:, t * P:(t + 1) * P], gate[:, 4 * g + t, :], ident[:])
                    mm.then_inc(gate_turned, 1)

            @block.scalar
            def _(act):
                act.wait_ge(args_ready, 1)
                act.activation(wts[:], raw[:, 0:2, :, :], ACT.Exp).then_inc(exps_ready, 1)
                act.wait_ge(rounds_ready, 1)
                n_rounds = act.value_load(rounds[0:1, 0:1], min_val=1, max_val=COLS // 8)
                with act.Fori(0, n_rounds) as r:
                    for i in range(8):
                        n = 8 * r + i
                        act.wait_ge(d_ready, n + 1)
                        act.activation(load[:, 0:H], d[:, 0, :], ACT.Exp)
                        act.activation(fade[:], d[:, 1, :], ACT.Exp).then_inc(w_ready, 1)
                act.wait_ge(g_var, 1)
                act.activation(t2[:], t1[:], ACT.Sqrt, bias=eps[:]).then_inc(g_std, 1)
                act.wait_ge(g_arg, 1)
                act.activation(gate[:], cmp[:], ACT.Exp).then_inc(g_exp, 1)

            @block.vector
            def _(dve):
                st = Steps(dve, step)

                def do(op):
                    st.done(op)
                    st.wait()

                dve.wait_ge(params_in, 16 * 5)
                do(dve.tensor_tensor(prod[:], features[:], a_s[:].unsqueeze(1).to_broadcast([P, HI, HE]), ALU.mult))
                dve.tensor_reduce(node[:, :, 0:H], he(prod[:]), AX.X, ALU.add).then_inc(node_ready, 1)
                dve.tensor_copy(node[:, :, H:NROW], features[:]).then_inc(node_ready, 1)
                dve.wait_ge(node_ready, 2)
                do(dve.tensor_tensor(prod[:], features[:], a_d[:].unsqueeze(1).to_broadcast([P, HI, HE]), ALU.mult))
                dve.tensor_reduce(state[:, :, 0:H], he(prod[:]), AX.X, ALU.add).then_inc(node_ready, 1)
                do(dve.tensor_scalar(has[:], counts[:], 0.0, None, ALU.is_gt))
                do(dve.tensor_scalar(has_neg[:], has[:], -1.0, BIG, ALU.add, ALU.mult))
                dve.wait_ge(last_in, 16)
                tgt, own = state[:, :, 0:H], node[:, :, 0:H]
                far = last[:, 0:H].unsqueeze(1).to_broadcast([P, HI, H])
                dve.wait_ge(node_ready, 3)
                do(dve.tensor_tensor(cand[:], far, has[:].unsqueeze(2).to_broadcast([P, HI, H]), ALU.mult))
                do(dve.tensor_tensor(cand[:], cand[:], has_neg[:].unsqueeze(2).to_broadcast([P, HI, H]), ALU.add))
                do(dve.tensor_tensor(state[:, :, MX:DEN], cand[:], own, ALU.max))
                do(dve.tensor_tensor(raw[:, 0, :, :], own, tgt, ALU.add))
                do(dve.tensor_tensor(raw[:, 1, :, :], far, tgt, ALU.add))
                do(dve.tensor_tensor(raw[:, 2, :, :], state[:, :, MX:DEN], tgt, ALU.add))
                do(dve.scalar_tensor_tensor(act3[:], raw[:], SLOPE, raw[:], ALU.mult, ALU.max))
                for n in range(2):
                    do(dve.tensor_tensor(raw[:, n, :, :], act3[:, n, :, :], act3[:, 2, :, :], ALU.subtract))
                dve.tensor_scalar(raw[:, 1, :, :], raw[:, 1, :, :], 0.0, None, ALU.min).then_inc(args_ready, 1)
                dve.wait_ge(exps_ready, 1)
                do(dve.tensor_tensor(wts[:, 1, :, :], wts[:, 1, :, :], counts[:].unsqueeze(2).to_broadcast([P, HI, H]),
                                     ALU.mult))
                do(dve.tensor_tensor(state[:, :, DEN:ACC], wts[:, 0, :, :], wts[:, 1, :, :], ALU.add))
                do(dve.tensor_tensor(he(part[:]), he(features[:]), hh(wts[:, 0, :, :]), ALU.mult))
                do(dve.tensor_tensor(he(prod[:]), last[:, H:NROW].rearrange("p (h e) -> p h e", h=H).unsqueeze(1)
                                     .to_broadcast([P, HI, H, E]), hh(wts[:, 1, :, :]), ALU.mult))
                dve.tensor_tensor(state[:, :, ACC:SROW], part[:], prod[:], ALU.add).then_inc(state_ready, 1)
                do(dve.tensor_scalar(some[:], keys[:], 0.0, None, ALU.is_gt))
                dve.tensor_reduce(num[:], some[:], AX.X, ALU.add).then_inc(num_ready, 1)
                dve.wait_ge(num_done, 1)
                do(dve.tensor_scalar(num_i[:], num_all[:], 7.0, 8.0, ALU.add, ALU.max))
                dve.tensor_scalar(rounds[:], num_i[:], 3, None, ALU.logical_shift_right).then_inc(rounds_ready, 1)
                dve.wait_ge(consts, 2)
                do(dve.tensor_copy(spare[:], spare_i[:]))
                dve.memset(eps[:], EPS)
                dve.sem_inc(prepared, 1)
                dve.wait_ge(rounds_ready, 1)
                n_rounds = dve.value_load(rounds[0:1, 0:1], min_val=1, max_val=COLS // 8)
                R1, R2 = 8 + 8 * 9, 8 * 5

                with dve.Fori(0, n_rounds) as r:
                    c2, c3 = Steps(dve, step2, r * R1), Steps(dve, step3, r * R2)

                    def do2(op):
                        c2.done(op)
                        c2.wait()

                    def do3(op):
                        c3.done(op)
                        c3.wait()

                    do2(dve.max(key8[:], keys[:]))
                    dve.sem_inc(waited, 1)
                    do2(dve.match_replace(keys[:], key8[:], keys[:], 0.0))
                    bits = key8[:].bitcast(I32)
                    do2(dve.tensor_scalar(tgt0_i[:], bits, M - 1, None, ALU.bitwise_and))
                    do2(dve.tensor_scalar(src_i[:], bits, NODE_BITS, M - 1, ALU.logical_shift_right, ALU.bitwise_and))
                    do2(dve.tensor_scalar(none8[:], key8[:], 0.0, None, ALU.is_equal))
                    do2(dve.tensor_scalar(spare8[:], none8[:], spare[:, 0:1], None, ALU.mult))
                    do2(dve.tensor_tensor(tgt_f[:], tgt0_i[:], spare8[:], ALU.add))
                    c2.done(dve.tensor_copy(tgt_i[:], tgt_f[:]))
                    c2.wait()
                    dve.sem_inc(decoded, 1)

                    def prepare(i):
                        n = 8 * r + i
                        dve.wait_ge(same_ready, n + 1)
                        do2(dve.tensor_scalar(same[i % 2][:], ps_same[:], tgt_f[:, i:i + 1], None, ALU.is_equal))
                        do2(dve.tensor_scalar(differ[:], same[i % 2][:], -1.0, BIG, ALU.add, ALU.mult))
                        do2(dve.tensor_tensor(scratch[:], same[i % 2][:], before[:], ALU.mult))
                        do2(dve.tensor_reduce(mates[:], scratch[:], AX.X, ALU.add))
                        do2(dve.tensor_scalar(away[:], mates[:], 0.0, None, ALU.is_gt))
                        do2(dve.tensor_tensor(step_f[:], spare[:], tgt_f[:, i:i + 1], ALU.subtract))
                        do2(dve.scalar_tensor_tensor(put_f[:], away[:], step_f[:, 0:1], tgt_f[:, i:i + 1],
                                                     ALU.mult, ALU.add))
                        do2(dve.tensor_copy(put_i[:, i:i + 1], put_f[:]))
                        dve.wait_ge(best_ready, n + 1)
                        do2(dve.tensor_tensor(masked[:], ps_best[:], differ[:].unsqueeze(1).to_broadcast([P, H, P]),
                                              ALU.add))
                        dve.tensor_reduce(best[i % 2][:], masked[:], AX.X, ALU.max).then_inc(prepared, 1)

                    def fold(i):
                        n = 8 * r + i
                        dve.wait_ge(prepared, n + 2)
                        dve.wait_ge(row_in, 16 * n + 16)
                        tgt1 = row[:, 0:H]
                        dve.tensor_copy(new[:, 0:H], tgt1)
                        dve.tensor_tensor(z[:, 0, :], src_row[:, i, 0:H], tgt1, ALU.add)
                        dve.tensor_tensor(z[:, 1, :], row[:, MX:DEN], tgt1, ALU.add)
                        do3(dve.tensor_tensor(new[:, MX:DEN], row[:, MX:DEN], best[i % 2][:], ALU.max))
                        do3(dve.tensor_tensor(z[:, 2, :], new[:, MX:DEN], tgt1, ALU.add))
                        do3(dve.scalar_tensor_tensor(zl[:], z[:], SLOPE, z[:], ALU.mult, ALU.max))
                        dve.tensor_tensor(d[:], zl[:, 0:2, :], zl[:, 2:3, :].to_broadcast([P, 2, H]), ALU.subtract
                                          ).then_inc(d_ready, 1)
                        dve.wait_ge(w_ready, n + 1)
                        dve.tensor_tensor(load[:, H:H + HE].rearrange("p (h e) -> p h e", h=H),
                                          src_row[:, i, H:NROW].rearrange("p (h e) -> p h e", h=H),
                                          load[:, 0:H].unsqueeze(2).to_broadcast([P, H, E]), ALU.mult
                                          ).then_inc(load_ready, 1)
                        do3(dve.tensor_tensor(kept[:, 0:H], row[:, DEN:ACC], fade[:], ALU.mult))
                        do3(dve.tensor_tensor(kept[:, H:H + HE].rearrange("p (h e) -> p h e", h=H),
                                              row[:, ACC:SROW].rearrange("p (h e) -> p h e", h=H),
                                              fade[:].unsqueeze(2).to_broadcast([P, H, E]), ALU.mult))
                        dve.wait_ge(sum_ready, n + 1)
                        dve.tensor_tensor(new[:, DEN:SROW], kept[:], ps_sum[:], ALU.add).then_inc(new_ready, 1)

                    prepare(0)
                    for i in range(8):
                        if i + 1 < 8:
                            prepare(i + 1)
                        fold(i)
                    dve.wait_ge(row_out, 16 * (8 * r + 7) + 16)

                dve.wait_ge(state_in, 16)
                dve.sem_inc(gate_kept, 2)
                do(dve.tensor_scalar(g1[:], state[:, :, DEN:ACC], 1e-16, None, ALU.add))
                do(dve.reciprocal(g2[:], g1[:]))
                do(dve.tensor_tensor(he(agg[:]), he(state[:, :, ACC:SROW]), hh(g2[:]), ALU.mult))
                wide = [vec[:, n, :].unsqueeze(1).to_broadcast([P, HI, HE]) for n in range(3)]
                do(dve.tensor_tensor(agg[:], agg[:], wide[0], ALU.add))
                do(dve.tensor_reduce(t1[:], agg[:], AX.X, ALU.add))
                do(dve.tensor_scalar(t1[:], t1[:], 1.0 / HE, None, ALU.mult))
                do(dve.tensor_tensor(agg[:], agg[:], t1[:].unsqueeze(2).to_broadcast([P, HI, HE]), ALU.subtract))
                do(dve.tensor_tensor(part[:], agg[:], agg[:], ALU.mult))
                do(dve.tensor_reduce(t1[:], part[:], AX.X, ALU.add))
                dve.tensor_scalar(t1[:], t1[:], 1.0 / HE, None, ALU.mult).then_inc(g_var, 1)
                dve.wait_ge(g_std, 1)
                do(dve.reciprocal(t1[:], t2[:]))
                do(dve.tensor_tensor(agg[:], agg[:], t1[:].unsqueeze(2).to_broadcast([P, HI, HE]), ALU.mult))
                do(dve.tensor_tensor(agg[:], agg[:], wide[1], ALU.mult))
                do(dve.tensor_tensor(agg[:], agg[:], wide[2], ALU.add))
                do(dve.tensor_reduce(score[:], agg[:].rearrange("p t (h e) -> p t e h", h=H), AX.X, ALU.add))
                do(dve.tensor_scalar(score[:], score[:], 1.0 / H, None, ALU.mult))
                do(dve.memset(rank[:], 0.0))
                for e in range(E):
                    for o in range(E):
                        if o != e:
                            do(dve.tensor_tensor(cmp[:, :, 0], score[:, :, o], score[:, :, e],
                                                 ALU.is_ge if o < e else ALU.is_gt))
                            do(dve.tensor_tensor(rank[:, :, e], rank[:, :, e], cmp[:, :, 0], ALU.add))
                do(dve.tensor_reduce(t1[:], score[:], AX.X, ALU.max))
                do(dve.tensor_scalar(rank[:], rank[:], 2.0, None, ALU.is_lt))
                dve.tensor_tensor(cmp[:], score[:], t1[:].unsqueeze(2).to_broadcast([P, HI, E]), ALU.subtract
                                  ).then_inc(g_arg, 1)
                dve.wait_ge(g_exp, 1)
                do(dve.tensor_tensor(gate[:], gate[:], rank[:], ALU.mult))
                do(dve.tensor_reduce(t1[:], gate[:], AX.X, ALU.add))
                do(dve.reciprocal(t2[:], t1[:]))
                dve.tensor_tensor(gate[:], gate[:], t2[:].unsqueeze(2).to_broadcast([P, HI, E]), ALU.mult
                                  ).then_inc(gate_ready, 1)
                for g in range(HI // 4):
                    dve.wait_ge(gate_turned, g + 1)
                    dve.tensor_copy(gate_t[:, g * 4 * P:(g + 1) * 4 * P], ps_gate[g % 2][:]).then_inc(gate_kept, 1)


def build(nc, x4, x3, conv, gains, shifts, table, w_out, b_out, w_gat, att_src, att_dst, b_gat, gamma, beta,
          w1, b1, w2, b2, edges, out):
    def dram(name, shape):
        return nc.dram_tensor(name, shape, F32, kind="Internal").ap()

    HE = w_gat.shape[1]
    H = att_src.shape[1]
    qkv = dram("qkv", (3, B, C, N))
    attended, x_mid, tokens = (dram(n, (B, C, N)) for n in ("attended", "x_mid", "tokens"))
    node_rows = dram("node_rows", (M, H + HE))
    state_rows = dram("state_rows", (M + P, 3 * H + HE))
    gates = dram("gates", (w1.shape[0], M))
    project(nc, x4, conv, gains, shifts, qkv)
    attend(nc, qkv, table, attended)
    with ExitStack() as ctx:
        features = ctx.enter_context(nc.sbuf_tensor("features", [P, HI, HE], F32))
        counts = ctx.enter_context(nc.sbuf_tensor("counts", [P, HI], F32))
        keys = ctx.enter_context(nc.sbuf_tensor("keys", [P, edges.shape[1] // P], F32))
        mix(nc, attended, x3, w_out, b_out, w_gat, x_mid, tokens, features)
        sort_edges(nc, edges, counts, keys)
        route(nc, features, counts, keys, att_src, att_dst, b_gat, gamma, beta, node_rows, state_rows, gates)
    experts(nc, tokens, x_mid, gates.rearrange("e (b n) -> e b n", b=B), w1, b1, w2, b2, out)


def kernel(x, L0_conv_Wq, L0_conv_gq, L0_conv_bq, L0_conv_Wk, L0_conv_gk, L0_conv_bk, L0_conv_Wv, L0_conv_gv,
           L0_conv_bv, L0_conv_bias_table, L0_conv_Wout, L0_conv_bout, L0_ffn_W_gat, L0_ffn_att_src,
           L0_ffn_att_dst, L0_ffn_b_gat, L0_ffn_ln_gamma, L0_ffn_ln_beta, L0_ffn_W1, L0_ffn_b1, L0_ffn_W2,
           L0_ffn_b2, L0_ffn_edge_index):
    import concourse.bacc as _bacc
    from concourse.bass_utils import run_bass_kernel_spmd as _run

    nc = _bacc.Bacc("TRN2", target_bir_lowering=False, num_devices=1)
    arrays = {}

    def take(name, a):
        a = np.ascontiguousarray(a)
        arrays[f"in_{name}"] = a
        return nc.dram_tensor(f"in_{name}", a.shape, mybir.dt.from_np(a.dtype), kind="ExternalInput").ap()

    def by_partition(a):
        return np.asarray(a).reshape(CT, P).T

    x = np.asarray(x)
    conv = [take(f"w{n}", np.asarray(w).transpose(1, 2, 3, 0).reshape(C, TAPS, C))
            for n, w in zip("qkv", (L0_conv_Wq, L0_conv_Wk, L0_conv_Wv))]
    gains = [take(f"g{n}", by_partition(g)) for n, g in zip("qkv", (L0_conv_gq, L0_conv_gk, L0_conv_gv))]
    shifts = [take(f"b{n}", by_partition(b)) for n, b in zip("qkv", (L0_conv_bq, L0_conv_bk, L0_conv_bv))]
    x4 = take("x", x)
    x3 = x4.rearrange("b c h w -> b c (h w)")
    table = take("table", np.asarray(L0_conv_bias_table).T.reshape(HEADS, 2 * IH - 1, 2 * IW - 1))
    w_out = take("w_out", np.asarray(L0_conv_Wout)[:, :, 0, 0].T)
    b_out = take("b_out", by_partition(L0_conv_bout))
    w_gat = take("w_gat", L0_ffn_W_gat)
    att = [take(n, np.asarray(a)[None]) for n, a in (("att_src", L0_ffn_att_src), ("att_dst", L0_ffn_att_dst))]
    rows = [take(n, np.asarray(a)[None]) for n, a in
            (("b_gat", L0_ffn_b_gat), ("gamma", L0_ffn_ln_gamma), ("beta", L0_ffn_ln_beta))]
    b1 = np.asarray(L0_ffn_b1)
    w1, w2 = take("w1", L0_ffn_W1), take("w2", L0_ffn_W2)
    b1 = take("b1", b1.reshape(b1.shape[0], -1, P).transpose(2, 0, 1))
    b2 = take("b2", L0_ffn_b2)
    edges = take("edges", L0_ffn_edge_index)
    out = nc.dram_tensor("out", (B, C, N), F32, kind="ExternalOutput").ap()
    build(nc, x4, x3, conv, gains, shifts, table, w_out, b_out, w_gat, *att, *rows, w1, b1, w2, b2, edges, out)
    return _run(nc, [arrays], core_ids=[0]).results[0]["out"].reshape(x.shape)
```

```python
from contextlib import ExitStack

import numpy as np

import concourse.bass as bass
from concourse import mybir

F32 = mybir.dt.float32
BF16 = mybir.dt.bfloat16
I32 = mybir.dt.int32
ALU = mybir.AluOpType
ACT = mybir.ActivationFunctionType
AX = mybir.AxisListType

P = 128
B, C, IH, IW = 8, 256, 32, 32
N = IH * IW
CT = C // P
HALF = 512
HALVES = N // HALF
HEADS, DH = 8, 32
SCALE = DH ** -0.5
PADW = IW + 2
TAPS = 9
M = B * N
BIG = 3.0e38
HI = M // P
KEY_BASE = 0x20000000


class Space:

    def __init__(self, nc, ctx, stage):
        self.nc, self.ctx, self.stage, self.sems = nc, ctx, stage, []
        ctx.callback(self.release)

    def sb(self, name, shape, dt=F32):
        return self.ctx.enter_context(self.nc.sbuf_tensor(f"{self.stage}_{name}", shape, dt))

    def ps(self, name, shape, dt=F32):
        return self.ctx.enter_context(self.nc.psum_tensor(f"{self.stage}_{name}", shape, dt))

    def sem(self, name):
        self.sems.append(self.nc.alloc_semaphore(f"{self.stage}_{name}"))
        return self.sems[-1]

    def release(self):
        self.nc.clear_and_free_semaphores(self.sems)
        self.nc.all_engine_barrier()


def project_and_sort(nc, x, weights, gains, shifts, qkv, edges, counts, keys):
    EPS_LN = EPS_PROJ = 1e-6
    GROUPS = 3 * CT * HALVES
    COLS = edges.shape[1] // P
    CHUNKS = GROUPS // 3
    CH = COLS // (B * CHUNKS)
    SUB = 32
    BLOCKS = CH // SUB
    NODE_BITS = M.bit_length() - 1
    LO_BITS = P.bit_length() - 1
    SPREAD = [-(-BLOCKS * g // 3) for g in range(4)]

    def slot(g):
        return range(SPREAD[g % 3], SPREAD[g % 3 + 1])

    with ExitStack() as ctx:
        s = Space(nc, ctx, "project")
        w = [s.sb(f"w{p}", [P, CT, TAPS, C]) for p in range(3)]
        gain = s.sb("gain", [P, 3, CT])
        shift = s.sb("shift", [P, 3, CT])
        ones_c = s.sb("ones_c", [P, P])
        ones_p = s.sb("ones_p", [P, P])
        x_in = [s.sb(f"x_in{i}", [P, CT, N]) for i in range(2)]
        xc = s.sb("xc", [P, CT, N])
        sq = s.sb("sq", [P, CT, N])
        rstd = s.sb("rstd", [P, N])
        eps = s.sb("eps", [P, 1])
        xn = [s.sb(f"xn{i}", [P, CT, IH + 2, PADW]) for i in range(2)]
        y = [s.sb(f"y{p}", [P, CT, N]) for p in range(3)]
        stats = s.sb("stats", [P, 3, CT * HALVES, 6])
        mv = s.sb("mv", [P, 3, 2])
        mean_s = s.sb("mean_s", [P, 3])
        dev = s.sb("dev", [P, 3])
        spread = s.sb("spread", [P, 3])
        y_std = s.sb("y_std", [P, 3])
        inv = s.sb("inv", [P, 3])
        a_scale = s.sb("a_scale", [P, 3, CT])
        a_prod = s.sb("a_prod", [P, 3, CT])
        a_bias = s.sb("a_bias", [P, 3, CT])
        ps_ln = s.ps("ps_ln", [P, HALVES, HALF])
        ps_conv = [s.ps(f"ps_conv{i}", [P, HALF]) for i in range(4)]
        ps_tiny = s.ps("ps_tiny", [P, 8])
        src, dst = s.sb("src", [P, CH], I32), s.sb("dst", [P, CH], I32)
        hi_i, lo_i, key_i = (s.sb(n, [P, CH], I32) for n in ("hi_i", "lo_i", "key_i"))
        m_src, m_dst, pen = (s.sb(n, [P, CH], I32) for n in ("m_src", "m_dst", "pen"))
        hi = s.sb("hi", [P, CH], BF16)
        lo = s.sb("lo", [P, CH], BF16)
        ramp_i = s.sb("ramp_i", [P, P], I32)
        ramp = s.sb("ramp", [P, P, SUB], BF16)
        hot_hi = [s.sb(f"hot_hi{i}", [P, HI, SUB], BF16) for i in range(2)]
        hot_lo = [s.sb(f"hot_lo{i}", [P, P, SUB], BF16) for i in range(2)]
        zero = s.sb("zero", [P, P], BF16)
        ps_count = s.ps("ps_count", [P, HI])

        params_in, consts = s.sem("params_in"), s.sem("consts")
        x_loaded = [s.sem(f"x_loaded{i}") for i in range(2)]
        mean_ready, centered, squared = s.sem("mean_ready"), s.sem("centered"), s.sem("squared")
        var_ready, rstd_ready, xn_ready = s.sem("var_ready"), s.sem("rstd_ready"), s.sem("xn_ready")
        conv_done, conv_copied, conv_stat = s.sem("conv_done"), s.sem("conv_copied"), s.sem("conv_stat")
        aggregated, m_ready, dev_done = s.sem("aggregated"), s.sem("m_ready"), s.sem("dev_done")
        spread_ready, v_ready, inv_done = s.sem("spread_ready"), s.sem("v_ready"), s.sem("inv_done")
        scale_done, prod_done = s.sem("scale_done"), s.sem("prod_done")
        affine_ready, gelu_done, q_done = s.sem("affine_ready"), s.sem("gelu_done"), s.sem("q_done")
        scaled_from, stdev_ready, y_std_ready = s.sem("scaled_from"), s.sem("stdev_ready"), s.sem("y_std_ready")
        aggr_may = s.sem("aggr_may")
        stored = [s.sem(f"stored{p}") for p in range(3)]
        edges_in, ramped, fields, masks, parsed = (s.sem(n) for n in ("edges_in", "ramped", "fields", "masks", "parsed"))
        hot, counted, all_counted, kept = s.sem("hot"), s.sem("counted"), s.sem("all_counted"), s.sem("kept")

        with nc.Block() as block:

            @block.sync
            def _(sp):
                def load_edges(c):
                    if not (isinstance(c, int) and c == 0):
                        sp.wait_ge(parsed, c)
                    for row, buf in ((0, src), (1, dst)):
                        sp.dma_start(buf[:], edges[row].rearrange("(p j) -> p j", p=P)[:, bass.ds(c * CH, CH)]
                                     ).then_inc(edges_in, 16)

                for p in range(3):
                    sp.dma_start(gain[:, p, :], gains[p]).then_inc(params_in, 16)
                    sp.dma_start(shift[:, p, :], shifts[p]).then_inc(params_in, 16)
                sp.dma_start(x_in[0][:], x[0].rearrange("(c p) h w -> p c (h w)", p=P)).then_inc(x_loaded[0], 16)
                for p in range(3):
                    sp.dma_start(w[p][:], weights[p].rearrange("(c p) t o -> p c t o", p=P)).then_inc(params_in, 16)

                def load_x(b, i):
                    sp.dma_start(x_in[i][:], x[bass.ds(b, 1)].rearrange("a (c p) h w -> p (a c) (h w)", p=P)
                                 ).then_inc(x_loaded[i], 16)

                def store(b, p):
                    sp.wait_ge(gelu_done if p else q_done, 2 * b + p if p else b + 1)
                    sp.dma_start(qkv[p, bass.ds(b, 1)].rearrange("a (c p) n -> p (a c) n", p=P), y[p][:]
                                 ).then_inc(stored[p], 16)

                def image(b, i, to_come):
                    c = CHUNKS * b
                    load_edges(c + 2)
                    store(b, 0)
                    load_edges(c + 3)
                    if to_come > 0:
                        load_edges(c + 4)
                    store(b, 1)
                    if to_come > 1:
                        sp.wait_ge(centered, b + 2)
                        load_x(b + 2, i)
                    if to_come > 0:
                        load_edges(c + 5)
                    store(b, 2)

                load_edges(0)
                load_edges(1)
                load_x(1, 1)
                image(0, 0, 2)
                image(1, 1, 2)
                with sp.Fori(1, B // 2 - 1) as it:
                    image(2 * it, 0, 2)
                    image(2 * it + 1, 1, 2)
                image(B - 2, 0, 1)
                image(B - 1, 1, 0)
                for p in range(3):
                    sp.wait_ge(stored[p], 16 * B)

            @block.gpsimd
            def _(pool):
                pool.iota(ramp_i[:], [[1, P]], base=0, channel_multiplier=0).then_inc(ramped, 1)

            @block.tensor
            def _(pe):
                def mean(b, i):
                    pe.wait_ge(x_loaded[i], 16 * (b // 2) + 16 if isinstance(b, int) else 8 * (b - i) + 16)
                    if not (isinstance(b, int) and b == 0):
                        pe.wait_ge(rstd_ready, b)
                    for half in range(HALVES):
                        for c in range(CT):
                            mm = pe.matmul(ps_ln[:, half, :], ones_c[:], x_in[i][:, c, half * HALF:(half + 1) * HALF],
                                           start=c == 0, stop=c == CT - 1)
                    mm.then_inc(mean_ready, 1)

                def variance(b):
                    pe.wait_ge(squared, b + 1)
                    for half in range(HALVES):
                        for c in range(CT):
                            mm = pe.matmul(ps_ln[:, half, :], ones_c[:], sq[:, c, half * HALF:(half + 1) * HALF],
                                           start=c == 0, stop=c == CT - 1)
                    mm.then_inc(var_ready, 1)

                def over_partitions(k, p, what):
                    if what == "mean":
                        pe.wait_ge(aggregated, k + 1)
                        pe.matmul(ps_tiny[:, p:p + 1], ones_p[:], mv[:, p, 0:1], start=True, stop=True
                                  ).then_inc(m_ready, 1)
                    else:
                        pe.wait_ge(spread_ready, k + 1)
                        pe.matmul(ps_tiny[:, 4 + p:5 + p], ones_p[:], spread[:, p:p + 1], start=True, stop=True
                                  ).then_inc(v_ready, 1)

                def count(c, n):
                    pe.wait_ge(hot, BLOCKS * c + n + 1)
                    for e in range(SUB):
                        mm = pe.matmul(ps_count[:], hot_lo[n % 2][:, :, e], hot_hi[n % 2][:, :, e],
                                       start=False, stop=False, skip_group_check=True)
                    mm.then_inc(counted, 1)

                def image(b, i, last):
                    pe.wait_ge(xn_ready, b + 1)
                    for g in range(GROUPS):
                        p, ct, half = g // 4, g // 2 % 2, g % 2
                        if not (isinstance(b, int) and b == 0 and g < 4):
                            pe.wait_ge(conv_copied, GROUPS * b + g - 3)
                        for c in range(CT):
                            for t in range(TAPS):
                                r0 = half * (IH // 2) + t // 3
                                mm = pe.matmul(ps_conv[g % 4][:], w[p][:, c, t, ct * P:(ct + 1) * P],
                                               xn[i][:, c, r0:r0 + IH // 2, t % 3:t % 3 + IW],
                                               start=c == 0 and t == 0, stop=c == CT - 1 and t == TAPS - 1)
                                for n in slot(g):
                                    if c * TAPS + t == TAPS + 4 * (n - slot(g)[0]):
                                        count(CHUNKS * b + g // 3, n)
                        mm.then_inc(conv_done, 1)
                        if g == 2 and not last:
                            mean(b + 1, 1 - i)
                        if g == 6 and not last:
                            variance(b + 1)
                        if g % 4 < 2 and not (isinstance(b, int) and b == 0 and p == 0):
                            over_partitions(3 * b + p - 1, (p - 1) % 3, "spread" if g % 4 else "mean")
                    if last:
                        over_partitions(3 * b + 2, 2, "mean")
                        over_partitions(3 * b + 2, 2, "spread")

                pe.wait_ge(consts, 7)
                pe.matmul(ps_count[:], zero[:], zero[:, 0:HI], start=True, stop=False, skip_group_check=True)
                mean(0, 0)
                variance(0)
                pe.wait_ge(params_in, 16 * 9)
                image(0, 0, False)
                image(1, 1, False)
                with pe.Fori(1, B // 2 - 1) as it:
                    image(2 * it, 0, False)
                    image(2 * it + 1, 1, False)
                image(B - 2, 0, False)
                image(B - 1, 1, True)
                pe.matmul(ps_count[:], zero[:], zero[:, 0:HI], start=False, stop=True, skip_group_check=True
                          ).then_inc(all_counted, 1)

            @block.vector
            def _(dve):
                dve.memset(ones_c[:], 1.0 / C).then_inc(consts, 1)
                dve.memset(ones_p[:], 1.0 / P).then_inc(consts, 1)
                dve.memset(eps[:], EPS_LN).then_inc(consts, 1)
                for i in range(2):
                    dve.memset(xn[i][:], 0.0).then_inc(consts, 1)

                dve.memset(zero[:], 0.0).then_inc(consts, 1)
                dve.wait_ge(ramped, 1)
                dve.tensor_copy(ramp[:], ramp_i[:].unsqueeze(2).to_broadcast([P, P, SUB])).then_inc(consts, 1)
                dve.sem_inc(counted, 2)

                def parse(c):
                    dve.wait_ge(edges_in, 32 * c + 32)
                    dve.tensor_scalar(hi_i[:], dst[:], LO_BITS, None, ALU.logical_shift_right).then_inc(fields, 1)
                    dve.tensor_scalar(lo_i[:], dst[:], P - 1, None, ALU.bitwise_and).then_inc(fields, 1)
                    dve.tensor_scalar(m_src[:], src[:], float(M - 1), -1.0, ALU.is_lt, ALU.mult).then_inc(fields, 1)
                    dve.tensor_scalar(m_dst[:], dst[:], float(M), -1.0, ALU.is_lt, ALU.mult).then_inc(fields, 1)
                    dve.tensor_scalar(pen[:], src[:], float(M - 1), float(HI), ALU.is_lt, ALU.mult).then_inc(fields, 1)
                    dve.tensor_scalar(key_i[:], src[:], NODE_BITS, KEY_BASE, ALU.logical_shift_left,
                                      ALU.bitwise_or).then_inc(fields, 1)
                    dve.wait_ge(fields, 6 * c + 6)
                    dve.tensor_tensor(m_dst[:], m_src[:], m_dst[:], ALU.bitwise_and).then_inc(masks, 1)
                    dve.tensor_tensor(key_i[:], key_i[:], dst[:], ALU.bitwise_or).then_inc(masks, 1)
                    dve.tensor_tensor(hi[:], hi_i[:], pen[:], ALU.add).then_inc(masks, 1)
                    dve.tensor_copy(lo[:], lo_i[:]).then_inc(masks, 1)
                    dve.wait_ge(masks, 4 * c + 4)
                    dve.tensor_tensor(keys[:].bitcast(I32)[:, bass.ds(c * CH, CH)], key_i[:], m_dst[:], ALU.bitwise_and
                                      ).then_inc(parsed, 1)

                def one_hot(c, n):
                    cols = slice(n * SUB, (n + 1) * SUB)
                    dve.wait_ge(counted, BLOCKS * c + n + 1)
                    dve.tensor_tensor(hot_hi[n % 2][:], ramp[:, 0:HI, :], hi[:, cols].unsqueeze(1).to_broadcast([P, HI, SUB]),
                                      ALU.is_equal)
                    dve.tensor_tensor(hot_lo[n % 2][:], ramp[:], lo[:, cols].unsqueeze(1).to_broadcast([P, P, SUB]),
                                      ALU.is_equal).then_inc(hot, 1)

                def center(b, i):
                    dve.wait_ge(mean_ready, b + 1)
                    if not (isinstance(b, int) and b == 0):
                        dve.wait_ge(xn_ready, b)
                    dve.tensor_tensor(xc[:, 0, :], x_in[i][:, 0, :], ps_ln[:].rearrange("p a b -> p (a b)"), ALU.subtract)
                    dve.tensor_tensor(xc[:, 1, :], x_in[i][:, 1, :], ps_ln[:].rearrange("p a b -> p (a b)"), ALU.subtract
                                      ).then_inc(centered, 1)

                def normalise(b, i):
                    dve.wait_ge(stdev_ready, b + 1)
                    dve.reciprocal(rstd[:], rstd[:]).then_inc(rstd_ready, 1)
                    dve.wait_ge(rstd_ready, b + 1)
                    if not (isinstance(b, int) and b < 2):
                        dve.wait_ge(conv_done, GROUPS * (b - 1))
                    for c in range(CT):
                        op = dve.tensor_tensor(xn[i][:, c, 1:1 + IH, 1:1 + IW],
                                               xc[:, c, :].rearrange("p (h w) -> p h w", w=IW),
                                               rstd[:].rearrange("p (h w) -> p h w", w=IW), ALU.mult)
                    op.then_inc(xn_ready, 1)

                def deviation(k, p):
                    dve.wait_ge(m_ready, k + 1)
                    dve.tensor_copy(mean_s[:, p:p + 1], ps_tiny[:, p:p + 1])
                    dve.tensor_tensor(dev[:, p:p + 1], mv[:, p, 0:1], ps_tiny[:, p:p + 1], ALU.subtract
                                      ).then_inc(dev_done, 1)
                    dve.wait_ge(dev_done, k + 1)
                    dve.scalar_tensor_tensor(spread[:, p:p + 1], dev[:, p:p + 1], dev[:, p:p + 1], mv[:, p, 1:2],
                                             ALU.mult, ALU.add).then_inc(spread_ready, 1)

                def affine(k, p):
                    dve.wait_ge(y_std_ready, k + 1)
                    dve.reciprocal(inv[:, p:p + 1], y_std[:, p:p + 1]).then_inc(inv_done, 1)
                    dve.wait_ge(inv_done, k + 1)
                    dve.tensor_scalar(a_scale[:, p, :], gain[:, p, :], inv[:, p:p + 1], None, ALU.mult
                                      ).then_inc(scale_done, 1)
                    dve.wait_ge(scale_done, k + 1)
                    dve.tensor_scalar(a_prod[:, p, :], a_scale[:, p, :], mean_s[:, p:p + 1], None, ALU.mult
                                      ).then_inc(prod_done, 1)
                    dve.wait_ge(prod_done, k + 1)
                    dve.tensor_tensor(a_bias[:, p, :], shift[:, p, :], a_prod[:, p, :], ALU.subtract
                                      ).then_inc(affine_ready, 1)

                def image(b, i, last):
                    for g in range(GROUPS):
                        p = g // 4
                        ct, half = g // 2 % 2, g % 2 if p == 0 else 1 - g % 2
                        c = CHUNKS * b + g // 3
                        if g % 3 == 0:
                            parse(c)
                        for n in slot(g):
                            one_hot(c, n)
                        dve.wait_ge(conv_copied, GROUPS * b + g + 1)
                        dve.bn_stats(stats[:, p, g % 4, :], y[p][:, ct, half * HALF:(half + 1) * HALF]
                                     ).then_inc(conv_stat, 1)
                        if g % 4 == 3:
                            dve.wait_ge(conv_stat, GROUPS * b + g + 1)
                            dve.sem_inc(aggr_may, 1)
                            dve.bn_aggr(mv[:, p, :], stats[:, p, :, :]).then_inc(aggregated, 1)
                        if g == 3 and not last:
                            center(b + 1, 1 - i)
                        if g == 7 and not last:
                            normalise(b + 1, 1 - i)
                        if g % 4 < 2 and not (isinstance(b, int) and b == 0 and p == 0):
                            (affine if g % 4 else deviation)(3 * b + p - 1, (p - 1) % 3)
                    if last:
                        deviation(3 * b + 2, 2)
                        affine(3 * b + 2, 2)

                dve.wait_ge(consts, 7)
                center(0, 0)
                normalise(0, 0)
                dve.wait_ge(params_in, 16 * 9)
                image(0, 0, False)
                image(1, 1, False)
                with dve.Fori(1, B // 2 - 1) as it:
                    image(2 * it, 0, False)
                    image(2 * it + 1, 1, False)
                image(B - 2, 0, False)
                image(B - 1, 1, True)
                dve.wait_ge(all_counted, 1)
                dve.tensor_copy(counts[:], ps_count[:]).then_inc(kept, 1)
                dve.wait_ge(kept, 1)

            @block.scalar
            def _(act):
                def square(b):
                    act.wait_ge(centered, b + 1)
                    if not (isinstance(b, int) and b == 0):
                        act.wait_ge(var_ready, b)
                    act.activation(sq[:], xc[:], ACT.Square).then_inc(squared, 1)

                def stdev_tokens(b):
                    act.wait_ge(var_ready, b + 1)
                    if not (isinstance(b, int) and b == 0):
                        act.wait_ge(xn_ready, b)
                    act.activation(rstd[:], ps_ln[:].rearrange("p a b -> p (a b)"), ACT.Sqrt, bias=eps[:]
                                   ).then_inc(stdev_ready, 1)

                def stdev_image(k, p):
                    act.wait_ge(v_ready, k + 1)
                    act.activation(y_std[:, p:p + 1], ps_tiny[:, 4 + p:5 + p], ACT.Sqrt, bias=eps[:]
                                   ).then_inc(y_std_ready, 1)

                def gelu(b, k, p):
                    act.wait_ge(affine_ready, k + 1)
                    for ct in range(CT):
                        op = act.activation(y[p][:, ct, :], y[p][:, ct, :], ACT.Gelu, bias=a_bias[:, p, ct:ct + 1],
                                            scale=a_scale[:, p, ct:ct + 1])
                    if p:
                        op.then_inc(gelu_done, 1)
                    else:
                        op.then_inc(scaled_from, 1)
                        act.wait_ge(scaled_from, b + 1)
                        act.activation(y[0][:], y[0][:], ACT.Copy, scale=SCALE).then_inc(q_done, 1)

                def image(b, last):
                    for g in range(GROUPS):
                        p, ct, half = g // 4, g // 2 % 2, g % 2
                        if g % 4 == 0 and not (isinstance(b, int) and b == 0):
                            act.wait_ge(stored[p], 16 * b)
                        act.wait_ge(conv_done, GROUPS * b + g + 1)
                        out = y[p][:, ct, half * HALF:(half + 1) * HALF] if p == 0 else y[p][:, ct, ::-1][
                            :, half * HALF:(half + 1) * HALF]
                        act.activation(out, ps_conv[g % 4][:], ACT.Copy).then_inc(conv_copied, 1)
                        if g == 4 and not last:
                            square(b + 1)
                        if g == 7 and not last:
                            stdev_tokens(b + 1)
                        if g % 4 in (1, 2) and not (isinstance(b, int) and b == 0 and p == 0):
                            if g % 4 == 1:
                                stdev_image(3 * b + p - 1, (p - 1) % 3)
                            else:
                                act.wait_ge(conv_copied, GROUPS * b + g + 1)
                                gelu(b, 3 * b + p - 1, (p - 1) % 3)
                    if last:
                        stdev_image(3 * b + 2, 2)
                        act.wait_ge(conv_copied, GROUPS * b + GROUPS)
                        gelu(b, 3 * b + 2, 2)

                act.wait_ge(consts, 5)
                square(0)
                stdev_tokens(0)
                image(0, False)
                image(1, False)
                with act.Fori(1, B // 2 - 1) as it:
                    image(2 * it, False)
                    image(2 * it + 1, False)
                image(B - 2, False)
                image(B - 1, True)


def attend(nc, qkv, table, attended):
    TILES = N // P
    BODY = 2 * TILES
    ROWS = P // IW
    U = IH + ROWS * (TILES - 1)
    KT = N // P
    QUART = KT // 2
    LAST = HEADS * B // 2 - 1
    F32R = mybir.dt.float32r
    with ExitStack() as ctx:
        s = Space(nc, ctx, "attend")
        bias = s.sb("bias", [P, U * IW])
        next_bias = s.sb("next_bias", [P, U * IW])
        q = [s.sb(f"q{j}", [4 * DH, N]) for j in range(2)]
        k = [s.sb(f"k{j}", [4 * DH, N]) for j in range(2)]
        q4 = [s.sb(f"q4{j}", [4 * DH, N], F32R) for j in range(2)]
        k4 = [s.sb(f"k4{j}", [4 * DH, N], F32R) for j in range(2)]
        v = [s.sb(f"v{j}", [DH, N]) for j in range(2)]
        vt = [s.sb(f"vt{j}", [P, KT, 2 * DH], F32R) for j in range(2)]
        neg = [s.sb(f"neg{j}", [P, N]) for j in range(2)]
        low = [s.sb(f"low{j}", [P, 1]) for j in range(2)]
        prob = [s.sb(f"prob{j}", [P, N]) for j in range(2)]
        sums = [s.sb(f"sums{j}", [P, TILES]) for j in range(2)]
        rs = s.sb("rs", [P, 4])
        rs_all = [s.sb(f"rs_all{j}", [P, 4, DH]) for j in range(2)]
        pth = [s.sb(f"pth{j}", [P, KT, HALF], F32R) for j in range(2)]
        ptl = [s.sb(f"ptl{j}", [P, KT, HALF], F32R) for j in range(2)]
        top = s.sb("top", [DH, HALF])
        both = s.sb("both", [DH, HALF])
        out = [s.sb(f"out{j}", [DH, HALF]) for j in range(2)]
        ident = s.sb("ident", [P, P])
        ps_s = [s.ps(f"ps_s{j}", [P, 2, HALF]) for j in range(2)]
        ps_t = [s.ps(f"ps_t{j}", [P, QUART, P]) for j in range(2)]
        ps_o = s.ps("ps_o", [2 * DH, HALF])
        ps_x = s.ps("ps_x", [P, HALF])
        ps_v = ps_x[:, 0:KT * DH].rearrange("p (t d) -> p t d", d=DH)
        ps_r = ps_x[:, KT * DH:KT * DH + P]

        consts, ident_zero = s.sem("consts"), s.sem("ident_zero")
        loaded = [s.sem(f"loaded{j}") for j in range(2)]
        v_loaded = [s.sem(f"v_loaded{j}") for j in range(2)]
        parts = s.sem("parts")
        r_count = s.sem("r_count")
        bias_loaded, bias_ready, waited = s.sem("bias_loaded"), s.sem("bias_ready"), s.sem("waited")
        h_count = [s.sem(f"h_count{j}") for j in range(2)]
        rs_count, vh_count, top_count, both_count = (s.sem(n) for n in ("rs_count", "vh_count", "top_count", "both_count"))
        stored = [s.sem(f"stored{j}") for j in range(2)]
        split, s_ready, v_ready = s.sem("split"), s.sem("s_ready"), s.sem("v_ready")
        neg_count, exp_count = s.sem("neg_count"), s.sem("exp_count")
        t_ready = [s.sem(f"t_ready{j}") for j in range(2)]
        l_count = [s.sem(f"l_count{j}") for j in range(2)]
        pv_count, out_count, vt_count = s.sem("pv_count"), s.sem("out_count"), s.sem("vt_count")
        CREDIT_NEG = CREDIT_EXP = CREDIT_SPLIT = CREDIT_V = 2
        CREDIT_T = [0, 2]
        CREDIT_S = 2 * TILES
        CREDIT_PV = 3
        CREDIT_L = CREDIT_VT = 1
        CREDIT_OUT = 2
        CREDIT_BOTH = 1

        def pipeline(eng, step, tail):
            for n in range(BODY):
                step(0, n, True)
            with eng.Fori(1, LAST + 1) as it:
                for n in range(BODY):
                    step(it, n, False)
            for n in range(BODY, BODY + tail):
                step(LAST, n, False)

        with nc.Block() as block:

            @block.sync
            def _(sp):
                def head_bias(h):
                    for yl in range(ROWS):
                        src = bass.AP(table.tensor, h * (2 * IH - 1) * (2 * IW - 1) + yl * (2 * IW - 1),
                                      [[1, IW], [2 * IW - 1, U], [1, IW]])
                        sp.dma_start(next_bias[yl * IW:(yl + 1) * IW, :], src).then_inc(bias_loaded, 16)

                def units(h, bp):
                    for j in range(2):
                        u = B * h + 2 * bp + j
                        sp.wait_ge(split, u + 1)
                        for p, dst in ((0, q), (1, k)):
                            src = bass.AP(qkv.tensor, p * B * C * N + (2 * bp + j) * C * N + h * DH * N,
                                          [[0, 4], [N, DH], [1, N]])
                            sp.dma_start(dst[j][:], src).then_inc(loaded[j], 16)
                        sp.wait_ge(v_ready, u + 1)
                        sp.dma_start(v[j][:], qkv[2, bass.ds(2 * bp + j, 1), bass.ds(h * DH, DH)].rearrange(
                            "a p n -> (a p) n")).then_inc(v_loaded[j], 16)

                head_bias(0)
                with sp.Fori(0, HEADS - 1) as h:
                    units(h, 0)
                    sp.wait_ge(bias_ready, h + 1)
                    head_bias(h + 1)
                    with sp.Fori(1, B // 2) as bp:
                        units(h, bp)
                with sp.Fori(0, B // 2) as bp:
                    units(HEADS - 1, bp)
                for j in range(2):
                    sp.wait_ge(stored[j], 16 * HEADS * B + 16)

            @block.gpsimd
            def _(pool):
                pool.sem_inc(split, CREDIT_SPLIT)
                pool.memset(ident[:], 0.0).then_inc(ident_zero, 1)
                pool.wait_ge(ident_zero, 1)
                pool.affine_select(out=ident[:], in_=ident[:], compare_op=ALU.not_equal, fill=1.0, base=0,
                                   pattern=[[-1, P]], channel_multiplier=1).then_inc(consts, 1)

                def split_unit(h, bp, j):
                    u = B * h + 2 * bp + j
                    pool.wait_ge(loaded[j], 32 * (B // 2 * h + bp) + 32)
                    pool.wait_ge(s_ready, TILES * (u + 1))
                    pool.sem_inc(waited, 1)
                    pool.tensor_copy(k4[j][:], k[j][:]).then_inc(parts, 1)
                    pool.wait_ge(parts, 4 * u + 1)
                    pool.sem_inc(waited, 1)
                    pool.tensor_copy(q4[j][:], q[j][:]).then_inc(parts, 1)
                    for n, g in enumerate((1, 3)):
                        rows = slice(g * DH, (g + 1) * DH)
                        pool.wait_ge(parts, 4 * u + 2 + n)
                        pool.tensor_tensor(k4[j][rows, :], k[j][rows, :], k4[j][rows, :].bitcast(F32), ALU.subtract
                                           ).then_inc(parts, 1)
                    pool.wait_ge(parts, 4 * u + 4)
                    pool.tensor_tensor(q4[j][2 * DH:, :], q[j][2 * DH:, :], q4[j][2 * DH:, :].bitcast(F32),
                                       ALU.subtract).then_inc(split, 1)
                    pool.wait_ge(split, u + 1 + CREDIT_SPLIT)
                    pool.sem_inc(waited, 1)

                with pool.Fori(0, HEADS) as h:
                    split_unit(h, 0, 0)
                    pool.wait_ge(bias_loaded, 16 * ROWS * (h + 1))
                    pool.wait_ge(neg_count, B * TILES * h + CREDIT_NEG)
                    pool.sem_inc(waited, 1)
                    pool.tensor_copy(bias[:], next_bias[:]).then_inc(bias_ready, 1)
                    pool.wait_ge(bias_ready, h + 1)
                    split_unit(h, 0, 1)
                    with pool.Fori(1, B // 2) as bp:
                        for j in range(2):
                            split_unit(h, bp, j)

            @block.tensor
            def _(pe):
                pe.sem_inc(s_ready, CREDIT_S)
                pe.sem_inc(v_ready, CREDIT_V)
                pe.sem_inc(t_ready[1], CREDIT_T[1])
                pe.sem_inc(pv_count, CREDIT_PV)

                def values(u, j):
                    pe.wait_ge(v_loaded[j], 8 * (u - j) + 16)
                    pe.wait_ge(out_count, 2 * u - 1 + CREDIT_OUT)
                    pe.sem_inc(waited, 1)
                    for kt in range(KT):
                        mm = pe.transpose(ps_v[:, kt, :], v[j][:, kt * P:(kt + 1) * P], ident[0:DH, 0:DH])
                    mm.then_inc(v_ready, 1)

                def scores(g, u, j, t):
                    if t == 0:
                        pe.wait_ge(split, u + 1 + CREDIT_SPLIT)
                    pe.wait_ge(neg_count, g + 1)
                    for half in range(2):
                        mm = pe.matmul(ps_s[t % 2][:, half, :], q4[j][:, t * P:(t + 1) * P],
                                       k4[j][:, half * HALF:(half + 1) * HALF], start=True, stop=True)
                    mm.then_inc(s_ready, 1)

                def turn(g, t):
                    pe.wait_ge(exp_count, g + 1 + CREDIT_EXP)
                    for bank in range(2):
                        pe.wait_ge(l_count[bank], g + CREDIT_L)
                        for i in range(QUART):
                            kt = bank * QUART + i
                            mm = pe.transpose(ps_t[bank][:, i, :], prob[t % 2][:, kt * P:(kt + 1) * P], ident[:])
                        mm.then_inc(t_ready[bank], 1)

                def weigh(m, u, j, half, quarter, next_u):
                    if quarter == 0:
                        for bank in range(2):
                            pe.wait_ge(l_count[bank], 4 * m + 4 + CREDIT_L)
                        pe.wait_ge(vt_count, u + 1 + CREDIT_VT)
                        pe.wait_ge(out_count, m + CREDIT_OUT)
                    for kt in range(2 * quarter, 2 * quarter + 2):
                        for part in (pth, ptl):
                            pe.matmul(ps_o[:], vt[j][:, kt, :], part[half][:, kt, :],
                                      start=kt == 0 and part is pth, stop=kt == KT - 1 and part is ptl)
                    if quarter == 3:
                        pe.wait_ge(rs_count, m + 1)
                        if next_u is not None:
                            pe.wait_ge(vt_count, next_u + 1 + CREDIT_VT)
                        pe.matmul(ps_r, rs_all[half][:].rearrange("p t d -> p (t d)"), ident[:],
                                  start=True, stop=True).then_inc(pv_count, 1)

                def step(it, n, first):
                    if n < BODY:
                        scores(BODY * it + n, 2 * it + n // TILES, n // TILES, n % TILES)
                    if not (first and n < 3) and n - 3 < BODY:
                        turn(BODY * it + n - 3, (n - 3) % 2)
                    if not (first and n < 7):
                        m, quarter = (n - 7) // 4, (n - 7) % 4
                        next_u = 2 * it + (m + 1) // 2 if m % 2 and m < 3 else None
                        weigh(4 * it + m, 2 * it + m // 2, m // 2 % 2, m % 2, quarter, next_u)
                    if n % TILES == 4 and n < BODY:
                        values(2 * it + n // TILES, n // TILES)

                pe.wait_ge(consts, 1)
                pipeline(pe, step, 7)

            @block.vector
            def _(dve):
                dve.sem_inc(neg_count, CREDIT_NEG)
                dve.sem_inc(l_count[0], CREDIT_L)
                dve.sem_inc(l_count[1], CREDIT_L)
                dve.sem_inc(vt_count, CREDIT_VT)
                dve.sem_inc(both_count, CREDIT_BOTH)
                dve.sem_inc(out_count, CREDIT_OUT)

                def values(u, j):
                    dve.wait_ge(v_ready, u + 1 + CREDIT_V)
                    dve.wait_ge(pv_count, 2 * u + 1)
                    dve.tensor_copy(vt[j][:, :, 0:DH], ps_v).then_inc(vh_count, 1)
                    dve.wait_ge(vh_count, u + 1)
                    dve.tensor_tensor(vt[j][:, :, DH:2 * DH], ps_v, vt[j][:, :, 0:DH].bitcast(F32), ALU.subtract
                                      ).then_inc(vt_count, 1)

                def negate(g, h, t):
                    if t == 0:
                        dve.wait_ge(bias_ready, h + 1)
                    dve.wait_ge(s_ready, g + 1 + CREDIT_S)
                    dve.wait_ge(exp_count, g + 1)
                    dve.sem_inc(waited, 1)
                    dve.tensor_tensor_reduce(neg[t % 2][:], ps_s[t % 2][:].rearrange("p a b -> p (a b)"),
                                             bias[:, t * P:t * P + N], -1.0, BIG, ALU.add, ALU.min, low[t % 2][:]
                                             ).then_inc(neg_count, 1)

                def lows(g, m, half, t):
                    dve.wait_ge(pv_count, m + 2)
                    for bank in range(2):
                        dve.wait_ge(h_count[bank], g + 1)
                        at = (slice(None), slice(bank * QUART, (bank + 1) * QUART), slice(t * P, (t + 1) * P))
                        dve.tensor_tensor(ptl[half][at], ps_t[bank][:], pth[half][at].bitcast(F32), ALU.subtract
                                          ).then_inc(l_count[bank], 1)

                def reciprocals(m, j, half):
                    dve.wait_ge(exp_count, 4 * m + 4 + CREDIT_EXP)
                    dve.wait_ge(pv_count, m + 2)
                    dve.reciprocal(rs[:], sums[j][:, half * 4:half * 4 + 4]).then_inc(r_count, 1)
                    dve.wait_ge(r_count, m + 1)
                    dve.tensor_copy(rs_all[half][:], rs[:].unsqueeze(2).to_broadcast([P, 4, DH])).then_inc(rs_count, 1)

                def finish(m, u, half):
                    dve.wait_ge(pv_count, m + 1 + CREDIT_PV)
                    dve.wait_ge(top_count, m + 1)
                    dve.tensor_tensor(both[:], ps_o[0:DH, :], top[:], ALU.add).then_inc(both_count, 1)
                    dve.wait_ge(both_count, m + 1 + CREDIT_BOTH)
                    dve.wait_ge(stored[half], 16 * u + 16)
                    for t in range(4):
                        cols = slice(t * P, (t + 1) * P)
                        op = dve.tensor_tensor(out[half][:, cols], both[:, cols], ps_r[t * DH:(t + 1) * DH, :], ALU.mult)
                    op.then_inc(out_count, 1)

                def step(it, n, first):
                    if n % TILES == 4 and n < BODY:
                        values(2 * it + n // TILES, n // TILES)
                    if n % 4 == 1 and not (first and n < 5) and n < BODY + 4:
                        m = (n - 5) // 4
                        reciprocals(4 * it + m, m // 2 % 2, m % 2)
                    if n < BODY:
                        negate(BODY * it + n, it // 4, n % TILES)
                    if n % 4 == 2 and not (first and n < 10):
                        m = (n - 10) // 4
                        finish(4 * it + m, 2 * it + m // 2, m % 2)
                    if not (first and n < 2) and n - 2 < BODY:
                        m = (n - 2) // 4
                        lows(BODY * it + n - 2, 4 * it + m, m % 2, (n - 2) % 4)

                dve.wait_ge(consts, 1)
                pipeline(dve, step, 7)

            @block.scalar
            def _(act):
                act.sem_inc(exp_count, CREDIT_EXP)
                for j in range(2):
                    act.sem_inc(stored[j], 16)

                def exps(g, j, t):
                    act.wait_ge(neg_count, g + 1 + CREDIT_NEG)
                    act.wait_ge(t_ready[1], g + 1)
                    act.activation(prob[t % 2][:], neg[t % 2][:], ACT.Exp, bias=low[t % 2][:], scale=-1.0,
                                   accum_out=sums[j][:, t:t + 1]).then_inc(exp_count, 1)

                def highs(g, m, half, t):
                    act.wait_ge(pv_count, m + 2)
                    for bank in range(2):
                        act.wait_ge(t_ready[bank], g + 1 + CREDIT_T[bank])
                        act.activation(pth[half][:, bank * QUART:(bank + 1) * QUART, t * P:(t + 1) * P], ps_t[bank][:],
                                       ACT.Copy).then_inc(h_count[bank], 1)

                def store(m, h, b, half):
                    act.wait_ge(out_count, m + 1 + CREDIT_OUT)
                    act.dma_start(attended[bass.ds(b, 1), bass.ds(h * DH, DH), half * HALF:(half + 1) * HALF
                                           ].rearrange("a p n -> (a p) n"), out[half][:]).then_inc(stored[half], 16)

                def lower(m):
                    act.wait_ge(pv_count, m + 1 + CREDIT_PV)
                    act.wait_ge(both_count, m + CREDIT_BOTH)
                    act.activation(top[:], ps_o[DH:2 * DH, :], ACT.Copy).then_inc(top_count, 1)

                def step(it, n, first):
                    if not (first and n < 1) and n - 1 < BODY:
                        exps(BODY * it + n - 1, (n - 1) // TILES % 2, (n - 1) % TILES)
                    if n % 4 == 2 and not (first and n < 10):
                        lower(4 * it + (n - 10) // 4)
                    if not (first and n < 2) and n - 2 < BODY:
                        m = (n - 2) // 4
                        highs(BODY * it + n - 2, 4 * it + m, m % 2, (n - 2) % 4)
                    if n % 4 == 3 and not (first and n < 11):
                        m = (n - 11) // 4
                        of = it if m >= 0 else it - 1
                        store(4 * it + m, of // 4, 2 * (of % 4) + m // 2 % 2, m % 2)

                pipeline(act, step, 8)


def mix(nc, attended, x, w_out, b_out, w_gat, x_mid, tokens, features):
    EPS = 1e-5
    KT = HALF // P
    NF = w_gat.shape[1]
    with ExitStack() as ctx:
        s = Space(nc, ctx, "mix")
        wo = s.sb("wo", [P, CT, C])
        wg = s.sb("wg", [P, CT, NF])
        bo = s.sb("bo", [P, CT])
        ones_c = s.sb("ones_c", [P, P])
        eps = s.sb("eps", [P, 1])
        att = [s.sb(f"att{i}", [P, CT, HALF]) for i in range(2)]
        xin = [s.sb(f"xin{i}", [P, CT, HALF]) for i in range(2)]
        mid = [s.sb(f"mid{i}", [P, CT, HALF]) for i in range(2)]
        cen = [s.sb(f"cen{i}", [P, CT, HALF]) for i in range(2)]
        sq = [s.sb(f"sq{i}", [P, CT, HALF]) for i in range(2)]
        stdev = [s.sb(f"stdev{i}", [P, HALF]) for i in range(2)]
        rstd = [s.sb(f"rstd{i}", [P, HALF]) for i in range(2)]
        tok = [s.sb(f"tok{i}", [P, CT, HALF]) for i in range(2)]
        ps_x = [s.ps(f"ps_x{i}", [P, CT, HALF]) for i in range(2)]
        ps_m = [s.ps(f"ps_m{i}", [P, HALF]) for i in range(2)]
        ps_h = [s.ps(f"ps_h{i}", [P, KT, NF]) for i in range(2)]
        params_in, consts, began = s.sem("params_in"), s.sem("consts"), s.sem("began")
        names = ("loaded", "projected", "summed", "mean_ready", "centered", "squared", "var_ready", "stdev_ready",
                 "rstd_ready", "tok_ready", "h_ready", "h_kept", "mid_stored", "tok_stored")
        (loaded, projected, summed, mean_ready, centered, squared, var_ready, stdev_ready, rstd_ready, tok_ready,
         h_ready, h_kept, mid_stored, tok_stored) = ([s.sem(f"{n}{i}") for i in range(2)] for n in names)

        with nc.Block() as block:

            @block.sync
            def _(sp):
                sp.dma_start(wo[:], w_out.rearrange("(c p) o -> p c o", p=P)).then_inc(params_in, 16)
                sp.dma_start(wg[:], w_gat.rearrange("(c p) o -> p c o", p=P)).then_inc(params_in, 16)
                sp.dma_start(bo[:], b_out).then_inc(params_in, 16)
                for i in range(2):
                    sp.sem_inc(summed[i], 1)
                with sp.Fori(0, B) as b:
                    for i in range(2):
                        sp.wait_ge(summed[i], b + 1)
                        for src, dst in ((attended, att), (x, xin)):
                            sp.dma_start(dst[i][:], src[bass.ds(b, 1), :, i * HALF:(i + 1) * HALF].rearrange(
                                "a (c p) n -> p (a c) n", p=P)).then_inc(loaded[i], 16)
                for i in range(2):
                    sp.wait_ge(mid_stored[i], 16 * B + 16)
                    sp.wait_ge(tok_stored[i], 16 * B + 16)

            @block.tensor
            def _(pe):
                pe.wait_ge(params_in, 48)
                pe.wait_ge(consts, 2)
                with pe.Fori(0, B) as b:
                    for i in range(2):
                        pe.wait_ge(loaded[i], 32 * b + 32)
                        pe.wait_ge(summed[i], b + 1)
                        for o in range(CT):
                            for c in range(CT):
                                mm = pe.matmul(ps_x[i][:, o, :], wo[:, c, o * P:(o + 1) * P], att[i][:, c, :],
                                               start=c == 0, stop=c == CT - 1)
                        mm.then_inc(projected[i], 1)
                    for i in range(2):
                        pe.wait_ge(summed[i], b + 2)
                        pe.wait_ge(stdev_ready[i], b + 1)
                        for c in range(CT):
                            mm = pe.matmul(ps_m[i][:], ones_c[:], mid[i][:, c, :], start=c == 0, stop=c == CT - 1)
                        mm.then_inc(mean_ready[i], 1)
                    for i in range(2):
                        pe.wait_ge(squared[i], b + 1)
                        for c in range(CT):
                            mm = pe.matmul(ps_m[i][:], ones_c[:], sq[i][:, c, :], start=c == 0, stop=c == CT - 1)
                        mm.then_inc(var_ready[i], 1)
                    for i in range(2):
                        pe.wait_ge(tok_ready[i], b + 1)
                        pe.wait_ge(h_kept[i], b + 1)
                        for t in range(KT):
                            for c in range(CT):
                                mm = pe.matmul(ps_h[i][:, t, :], tok[i][:, c, t * P:(t + 1) * P], wg[:, c, :],
                                               start=c == 0, stop=c == CT - 1)
                        mm.then_inc(h_ready[i], 1)

            @block.vector
            def _(dve):
                dve.memset(ones_c[:], 1.0 / C).then_inc(consts, 1)
                dve.memset(eps[:], EPS).then_inc(consts, 1)
                for i in range(2):
                    dve.sem_inc(h_kept[i], 1)
                dve.wait_ge(params_in, 48)
                with dve.Fori(0, B) as b:
                    for i in range(2):
                        dve.wait_ge(projected[i], b + 1)
                        dve.wait_ge(mid_stored[i], 16 * b + 16)
                        for o in range(CT):
                            op = dve.scalar_tensor_tensor(mid[i][:, o, :], ps_x[i][:, o, :], bo[:, o:o + 1],
                                                          xin[i][:, o, :], ALU.add, ALU.add)
                        op.then_inc(summed[i], 1)
                    for i in range(2):
                        dve.wait_ge(mean_ready[i], b + 1)
                        for c in range(CT):
                            op = dve.tensor_tensor(cen[i][:, c, :], mid[i][:, c, :], ps_m[i][:], ALU.subtract)
                        op.then_inc(centered[i], 1)
                    for i in range(2):
                        dve.wait_ge(stdev_ready[i], b + 2)
                        dve.reciprocal(rstd[i][:], stdev[i][:]).then_inc(rstd_ready[i], 1)
                        dve.wait_ge(rstd_ready[i], b + 1)
                        dve.wait_ge(tok_stored[i], 16 * b + 16)
                        for c in range(CT):
                            op = dve.tensor_tensor(tok[i][:, c, :], cen[i][:, c, :], rstd[i][:], ALU.mult)
                        op.then_inc(tok_ready[i], 1)
                    for i in range(2):
                        dve.wait_ge(h_ready[i], b + 1)
                        dve.tensor_copy(features[:, bass.ds(b * 2 * KT + i * KT, KT), :], ps_h[i][:]
                                        ).then_inc(h_kept[i], 1)

            @block.scalar
            def _(act):
                for i in range(2):
                    act.sem_inc(mid_stored[i], 16)
                    act.sem_inc(tok_stored[i], 16)
                    act.sem_inc(stdev_ready[i], 1)
                act.wait_ge(consts, 2)
                with act.Fori(0, B) as b:
                    for i in range(2):
                        act.wait_ge(summed[i], b + 2)
                        act.dma_start(x_mid[bass.ds(b, 1), :, i * HALF:(i + 1) * HALF].rearrange(
                            "a (c p) n -> p (a c) n", p=P), mid[i][:]).then_inc(mid_stored[i], 16)
                    for i in range(2):
                        act.wait_ge(centered[i], b + 1)
                        act.activation(sq[i][:], cen[i][:], ACT.Square).then_inc(squared[i], 1)
                    for i in range(2):
                        act.wait_ge(var_ready[i], b + 1)
                        act.activation(stdev[i][:], ps_m[i][:], ACT.Sqrt, bias=eps[:]).then_inc(stdev_ready[i], 1)
                    for i in range(2):
                        act.wait_ge(tok_ready[i], b + 1)
                        act.dma_start(tokens[bass.ds(b, 1), :, i * HALF:(i + 1) * HALF].rearrange(
                            "a (c p) n -> p (a c) n", p=P), tok[i][:]).then_inc(tok_stored[i], 16)


def experts(nc, tokens, x_mid, gates, w1, b1, w2, b2, out):
    E, _, F = w1.shape
    FT = F // P
    F32R = mybir.dt.float32r
    with ExitStack() as ctx:
        s = Space(nc, ctx, "experts")
        w1s = s.sb("w1", [P, E, CT, F])
        w2s = s.sb("w2", [P, E, FT, C])
        w1_high, w1_low = s.sb("w1_high", [P, E, CT, F], F32R), s.sb("w1_low", [P, E, CT, F], F32R)
        w2_high, w2_low = s.sb("w2_high", [P, E, FT, C], F32R), s.sb("w2_low", [P, E, FT, C], F32R)
        b1s = s.sb("b1", [P, E, FT])
        b2s = s.sb("b2", [E, C])
        tok = [s.sb(f"tok{i}", [P, CT, HALF]) for i in range(2)]
        tok_high = [s.sb(f"tok_high{i}", [P, CT, HALF], F32R) for i in range(2)]
        tok_low = [s.sb(f"tok_low{i}", [P, CT, HALF], F32R) for i in range(2)]
        mid = [s.sb(f"mid{i}", [P, CT, HALF]) for i in range(2)]
        gate = [s.sb(f"gate{i}", [E, HALF]) for i in range(2)]
        gate_all = [s.sb(f"gate_all{i}", [P, E, HALF]) for i in range(2)]
        hid = s.sb("hid", [P, FT, HALF])
        gated = s.sb("gated", [P, FT, HALF])
        hid_high = [s.sb(f"hid_high{j}", [P, FT, HALF], F32R) for j in range(2)]
        hid_low = [s.sb(f"hid_low{j}", [P, FT, HALF], F32R) for j in range(2)]
        res = s.sb("res", [P, CT, HALF])
        ps_h = [s.ps(f"ps_h{t}", [P, HALF]) for t in range(FT)]
        ps_y = s.ps("ps_y", [P, CT, HALF])
        params_in, w_high, w_split = s.sem("params_in"), s.sem("w_high"), s.sem("w_split")
        loaded = [s.sem(f"loaded{i}") for i in range(2)]
        tok_highs, tok_split, waited = s.sem("tok_highs"), s.sem("tok_split"), s.sem("waited")
        h_ready, h_gelu, h_gated, h_high, h_split = (
            s.sem(n) for n in ("h_ready", "h_gelu", "h_gated", "h_high", "h_split"))
        y_part, y_done, stored = s.sem("y_part"), s.sem("y_done"), s.sem("stored")

        with nc.Block() as block:

            @block.sync
            def _(sp):
                sp.dma_start(w1s[:], w1.rearrange("e (c p) f -> p e c f", p=P)).then_inc(params_in, 16)
                sp.dma_start(w2s[:], w2.rearrange("e (t p) o -> p e t o", p=P)).then_inc(params_in, 16)
                sp.dma_start(b1s[:], b1).then_inc(params_in, 16)
                sp.dma_start(b2s[:], b2).then_inc(params_in, 16)
                sp.sem_inc(y_done, 2)
                with sp.Fori(0, B) as b:
                    for i in range(2):
                        sp.wait_ge(y_done, 2 * b + i + 1)
                        cols = slice(i * HALF, (i + 1) * HALF)
                        for src, dst in ((tokens, tok), (x_mid, mid)):
                            sp.dma_start(dst[i][:], src[bass.ds(b, 1), :, cols].rearrange(
                                "a (c p) n -> p (a c) n", p=P)).then_inc(loaded[i], 16)
                        sp.dma_start(gate[i][:], gates[:, bass.ds(b, 1), cols].rearrange("e a n -> e (a n)")
                                     ).then_inc(loaded[i], 16)
                        sp.dma_start(gate_all[i][:], bass.AP(gates.tensor, b * N + i * HALF, [[0, P], [M, E], [1, HALF]])
                                     ).then_inc(loaded[i], 16)
                sp.wait_ge(stored, 16 * 2 * B + 16)

            @block.gpsimd
            def _(pool):
                with pool.Fori(0, B) as b:
                    for i in range(2):
                        pool.wait_ge(loaded[i], 64 * b + 64)
                        pool.sem_inc(waited, 1)
                        pool.tensor_copy(tok_high[i][:], tok[i][:]).then_inc(tok_highs, 1)
                        pool.wait_ge(tok_highs, 2 * b + i + 1)
                        pool.tensor_tensor(tok_low[i][:], tok[i][:], tok_high[i][:].bitcast(F32), ALU.subtract
                                           ).then_inc(tok_split, 1)
                        pool.wait_ge(tok_split, 2 * b + i + 1)
                        pool.sem_inc(waited, 1)

            @block.tensor
            def _(pe):
                def hidden(n, e, i):
                    parts = ((w1_high, tok_high[i]), (w1_high, tok_low[i]), (w1_low, tok_high[i]))
                    for t in range(FT):
                        pe.wait_ge(h_gelu, FT * n + t + 1)
                        for c in range(CT):
                            for m, (w, x) in enumerate(parts):
                                mm = pe.matmul(ps_h[t][:], w[:, e, c, t * P:(t + 1) * P], x[:, c, :],
                                               start=c == 0 and m == 0, stop=c == CT - 1 and m == 2)
                        mm.then_inc(h_ready, 1)

                def output(n, e):
                    high, low = hid_high[e % 2], hid_low[e % 2]
                    for t in range(FT):
                        pe.wait_ge(h_split, FT * n + t + 1 + FT)
                        for o in range(CT):
                            for w, h in ((w2_high, high), (w2_high, low), (w2_low, high)):
                                mm = pe.matmul(ps_y[:, o, :], w[:, e, t, o * P:(o + 1) * P], h[:, t, :],
                                               start=False, stop=False, skip_group_check=True)
                    mm.then_inc(y_part, 1)

                pe.wait_ge(w_split, 2)
                pe.sem_inc(y_part, 2)
                with pe.Fori(0, B) as b:
                    for i in range(2):
                        c0 = 2 * b + i
                        pe.wait_ge(tok_split, c0 + 1)
                        hidden(E * c0, 0, i)
                        pe.wait_ge(y_done, c0 + 2)
                        for o in range(CT):
                            pe.matmul(ps_y[:, o, :], b2s[:, o * P:(o + 1) * P], gate[i][:], start=True, stop=False,
                                      skip_group_check=True)
                        for e in range(E):
                            if e + 1 < E:
                                hidden(E * c0 + e + 1, e + 1, i)
                            output(E * c0 + e, e)

            @block.scalar
            def _(act):
                act.sem_inc(h_gelu, FT)
                act.sem_inc(stored, 16)
                act.wait_ge(params_in, 64)
                act.activation(w1_high[:], w1s[:], ACT.Copy).then_inc(w_high, 1)
                act.activation(w2_high[:], w2s[:], ACT.Copy).then_inc(w_high, 1)

                def high(n, e, t):
                    act.wait_ge(y_part, n + 1)
                    act.wait_ge(h_gated, FT * n + t + 1 + FT)
                    act.activation(hid_high[e % 2][:, t, :], gated[:, t, :], ACT.Copy).then_inc(h_high, 1)

                with act.Fori(0, B) as b:
                    for i in range(2):
                        c0 = 2 * b + i
                        for e in range(E):
                            n = E * c0 + e
                            for t in range(FT):
                                act.wait_ge(h_ready, FT * n + t + 1)
                                act.wait_ge(h_gated, FT * n + t + 1)
                                act.activation(hid[:, t, :], ps_h[t][:], ACT.Gelu, bias=b1s[:, e, t:t + 1]
                                               ).then_inc(h_gelu, 1)
                                if t:
                                    high(n, e, t - 1)
                            high(n, e, FT - 1)
                        act.wait_ge(y_done, c0 + 3)
                        act.dma_start(out[bass.ds(b, 1), :, i * HALF:(i + 1) * HALF].rearrange(
                            "a (c p) n -> p (a c) n", p=P), res[:]).then_inc(stored, 16)

            @block.vector
            def _(dve):
                dve.sem_inc(h_gated, FT)
                dve.sem_inc(h_split, FT)
                dve.wait_ge(w_high, 1)
                dve.tensor_tensor(w1_low[:], w1s[:], w1_high[:].bitcast(F32), ALU.subtract).then_inc(w_split, 1)
                dve.wait_ge(w_high, 2)
                dve.tensor_tensor(w2_low[:], w2s[:], w2_high[:].bitcast(F32), ALU.subtract).then_inc(w_split, 1)

                def low(n, e, t):
                    dve.wait_ge(h_high, FT * n + t + 1)
                    dve.tensor_tensor(hid_low[e % 2][:, t, :], gated[:, t, :], hid_high[e % 2][:, t, :].bitcast(F32),
                                      ALU.subtract).then_inc(h_split, 1)

                with dve.Fori(0, B) as b:
                    for i in range(2):
                        c0 = 2 * b + i
                        dve.wait_ge(loaded[i], 64 * b + 64)
                        for e in range(E):
                            n = E * c0 + e
                            for t in range(FT):
                                dve.wait_ge(h_gelu, FT * n + t + 1 + FT)
                                dve.wait_ge(h_split, FT * n + t + 1)
                                dve.tensor_tensor(gated[:, t, :], hid[:, t, :], gate_all[i][:, e, :], ALU.mult
                                                  ).then_inc(h_gated, 1)
                                if t:
                                    low(n, e, t - 1)
                            low(n, e, FT - 1)
                        dve.wait_ge(y_part, E * c0 + E + 2)
                        dve.wait_ge(stored, 16 * c0 + 16)
                        dve.tensor_tensor(res[:], ps_y[:], mid[i][:], ALU.add).then_inc(y_done, 1)

class Steps:

    def __init__(self, eng, sem, base=0):
        self.eng, self.sem, self.n = eng, sem, base

    def done(self, op):
        self.n = self.n + 1
        return op.then_inc(self.sem, 1)

    def wait(self):
        self.eng.wait_ge(self.sem, self.n)


def route(nc, features, counts, keys, att_src, att_dst, b_gat, gamma, beta, node_rows, state_rows, gates):
    H, E = att_src.shape[1], att_src.shape[2]
    HE = H * E
    NROW = H + HE
    SROW = 3 * H + HE
    MX, DEN, ACC = H, 2 * H, 3 * H
    SLOPE = 0.2
    EPS = 1e-5
    NODE_BITS = M.bit_length() - 1
    COLS = keys.shape[1]
    T = state_rows.shape[0]
    TABLE = M + P
    LO_BITS = P.bit_length() - 1
    HI_BITS = HI.bit_length() - 1
    BANKS = 5
    with ExitStack() as ctx:
        s = Space(nc, ctx, "route")
        a_s, a_d = s.sb("a_s", [P, HE]), s.sb("a_d", [P, HE])
        vec = s.sb("vec", [P, 3, HE])
        prod = s.sb("prod", [P, HI, HE])
        node = s.sb("node", [P, HI, NROW])
        state = s.sb("state", [P, HI, SROW])
        last = s.sb("last", [P, NROW])
        has = s.sb("has", [P, HI])
        has_neg = s.sb("has_neg", [P, HI])
        cand = s.sb("cand", [P, HI, H])
        raw = s.sb("raw", [P, 3, HI, H])
        act3 = s.sb("act3", [P, 3, HI, H])
        wts = s.sb("wts", [P, 2, HI, H])
        part = s.sb("part", [P, HI, HE])
        some = s.sb("some", [P, COLS], BF16)
        num = s.sb("num", [P, 1])
        num_all = s.sb("num_all", [P, 1])
        num_i = s.sb("num_i", [P, 1], I32)
        rounds = s.sb("rounds", [P, 1], I32)
        spare_i, base_i = s.sb("spare_i", [P, T], I32), s.sb("base_i", [P, T], I32)
        spare = s.sb("spare", [P, T])
        base = s.sb("base", [P, T])
        ident0, ident = s.sb("ident0", [P, P]), s.sb("ident", [P, P])
        ones = s.sb("ones", [P, P])
        ident_b = s.sb("ident_b", [P, P], BF16)
        before = s.sb("before", [P, P])
        nothing = s.sb("nothing", [P, HI, SROW])
        key8 = s.sb("key8", [P, T])
        none8, spare8, sum8, tgt_f = (s.sb(n, [P, T]) for n in ("none8", "spare8", "sum8", "tgt_f"))
        t_lo, t_hi, s_lo, s_hi, tgt0_i, src_i, tgt_i, put_i = (
            s.sb(n, [P, T], I32) for n in ("t_lo", "t_hi", "s_lo", "s_hi", "tgt0_i", "src_i", "tgt_i", "put_i"))
        src_row = s.sb("src_row", [P, T, NROW])
        same = s.sb("same", [P, T, P])
        differ = s.sb("differ", [P, T, P], BF16)
        scratch = s.sb("scratch", [P, T, P])
        mates, away, step_f, put_f = (s.sb(n, [P, T]) for n in ("mates", "away", "step_f", "put_f"))
        best = s.sb("best", [P, T, H])
        row = s.sb("row", [P, T, SROW])
        new = s.sb("new", [P, T, SROW])
        z, zl, d = s.sb("z", [P, 3, T, H]), s.sb("zl", [P, 3, T, H]), s.sb("d", [P, 2, T, H])
        load = s.sb("load", [P, T, H + HE])
        fade = s.sb("fade", [P, T, H])
        kept = s.sb("kept", [P, T, H + HE])
        tables = s.sb("tables", [P, T, HI, SROW])
        zt = s.sb("zt", [P, T + 1, HI, H])
        zt_l = s.sb("zt_l", [P, T + 1, HI, H])
        share = s.sb("share", [P, T, HI, H])
        agg = s.sb("agg", [P, HI, HE])
        g1, g2 = s.sb("g1", [P, HI, H]), s.sb("g2", [P, HI, H])
        t1, t2 = s.sb("t1", [P, HI]), s.sb("t2", [P, HI])
        eps = s.sb("eps", [P, 1])
        score, rank, cmp = s.sb("score", [P, HI, E]), s.sb("rank", [P, HI, E]), s.sb("cmp", [P, HI, E])
        gate = s.sb("gate", [P, HI, E])
        gate_t = tables[0:E, :, :, :].rearrange("p s t r -> p (s t r)")[:, 0:M]
        ps_same = s.ps("ps_same", [P, T, P])
        ps_best = [s.ps(f"ps_best{j}", [P, H, P]) for j in range(BANKS)]
        ps_sum = s.ps("ps_sum", [P, T, H + HE])
        ps_gate = [ps_best[j][0:E, :, :] for j in range(2)]

        params_in, consts, seeded = s.sem("params_in"), s.sem("consts"), s.sem("seeded")
        node_ready, node_out, last_in = s.sem("node_ready"), s.sem("node_out"), s.sem("last_in")
        args_ready, exps_ready, state_ready, state_out = (
            s.sem(n) for n in ("args_ready", "exps_ready", "state_ready", "state_out"))
        num_ready, num_done, rounds_ready = s.sem("num_ready"), s.sem("num_done"), s.sem("rounds_ready")
        step, step2, step3 = s.sem("step"), s.sem("step2"), s.sem("step3")
        decoded, round_done = s.sem("decoded"), s.sem("round_done")
        src_in = [s.sem(f"src_in{i}") for i in range(T)]
        row_out = [s.sem(f"row_out{i}") for i in range(T)]
        same_ready, differ_ready, best_ready, best_kept = (
            s.sem(n) for n in ("same_ready", "differ_ready", "best_ready", "best_kept"))
        row_in, d_ready, w_ready, load_ready = (s.sem(n) for n in ("row_in", "d_ready", "w_ready", "load_ready"))
        sum_ready, new_ready, waited = (s.sem(n) for n in ("sum_ready", "new_ready", "waited"))
        state_in, gate_ready, gate_turned, gate_kept, gate_out = (
            s.sem(n) for n in ("state_in", "gate_ready", "gate_turned", "gate_kept", "gate_out"))
        share_arg, share_exp = s.sem("share_arg"), s.sem("share_exp")
        g_var, g_std, g_arg, g_exp = (s.sem(n) for n in ("g_var", "g_std", "g_arg", "g_exp"))

        def hh(ap):
            return ap.unsqueeze(3).to_broadcast([P, HI, H, E])

        def he(ap):
            return ap.rearrange("p t (h e) -> p t h e", h=H)

        with nc.Block() as block:

            @block.sync
            def _(sp):
                sp.dma_start(a_s[:], att_src.rearrange("a h e -> a (h e)").to_broadcast([P, HE])).then_inc(params_in, 16)
                sp.dma_start(a_d[:], att_dst.rearrange("a h e -> a (h e)").to_broadcast([P, HE])).then_inc(params_in, 16)
                for n, v in enumerate((b_gat, gamma, beta)):
                    sp.dma_start(vec[:, n, :], v.to_broadcast([P, HE])).then_inc(params_in, 16)
                sp.wait_ge(node_ready, 3)
                sp.dma_start(node_rows.rearrange("(p t) r -> p (t r)", p=P), node[:].rearrange("p t r -> p (t r)")).then_inc(node_out, 16)
                sp.wait_ge(node_out, 16)
                sp.dma_start(last[:], node_rows[M - 1:M, :].to_broadcast([P, NROW])).then_inc(last_in, 16)
                sp.wait_ge(state_ready, 1)
                for i in range(T):
                    first = state if i == 0 else nothing
                    sp.dma_start(state_rows[i, 0:M, :].rearrange("(p t) r -> p (t r)", p=P),
                                 first[:].rearrange("p t r -> p (t r)")).then_inc(state_out, 16)
                    sp.dma_start(state_rows[i, M:TABLE, :], first[:, 0, :]).then_inc(state_out, 16)
                sp.wait_ge(round_done, 1)
                for i in range(T):
                    sp.dma_start(tables[:, i, :, :].rearrange("p t r -> p (t r)"),
                                 state_rows[i, 0:M, :].rearrange("(p t) r -> p (t r)", p=P)).then_inc(state_in, 16)
                sp.wait_ge(gate_kept, HI // 4 + 2)
                sp.dma_start(gates, gate_t).then_inc(gate_out, 16)
                sp.wait_ge(gate_out, 16)

            @block.gpsimd
            def _(pool):
                pool.iota(spare_i[:], [[TABLE, T]], base=M, channel_multiplier=1).then_inc(consts, 1)
                pool.iota(base_i[:], [[TABLE, T]], base=0, channel_multiplier=0).then_inc(consts, 1)
                pool.memset(ident0[:], 0.0).then_inc(seeded, 1)
                pool.memset(ones[:], 1.0).then_inc(seeded, 1)
                pool.wait_ge(seeded, 2)
                pool.affine_select(out=ident[:], in_=ident0[:], compare_op=ALU.not_equal, fill=1.0, base=0,
                                   pattern=[[-1, P]], channel_multiplier=1).then_inc(consts, 1)
                pool.affine_select(out=before[:], in_=ones[:], compare_op=ALU.is_gt, fill=0.0, base=0,
                                   pattern=[[-1, P]], channel_multiplier=1).then_inc(consts, 1)
                pool.wait_ge(num_ready, 1)
                pool.partition_all_reduce(num_all[:], num[:], P, bass.bass_isa.ReduceOp.max).then_inc(num_done, 1)
                pool.wait_ge(state_out, 32 * T)
                pool.wait_ge(rounds_ready, 1)
                n_rounds = pool.value_load(rounds[0:1, 0:1], min_val=1, max_val=COLS // 8)
                states = state_rows.rearrange("t m r -> (t m) r")

                def sources(r):
                    pool.wait_ge(decoded, r + 1)
                    pool.sem_inc(waited, 1)
                    for i in range(T):
                        pool.indirect_dma_start(src_row[:, i, :], None, node_rows,
                                                bass.IndirectOffsetOnAxis(src_i[:, i:i + 1], 0)).then_inc(src_in[i], 16)

                sources(0)
                with pool.Fori(0, n_rounds) as r:
                    for i in range(T):
                        pool.indirect_dma_start(row[:, i, :], None, states,
                                                bass.IndirectOffsetOnAxis(tgt_i[:, i:i + 1], 0)).then_inc(row_in, 16)
                    pool.wait_ge(new_ready, r + 1)
                    pool.sem_inc(waited, 1)
                    for i in range(T):
                        pool.indirect_dma_start(states, bass.IndirectOffsetOnAxis(put_i[:, i:i + 1], 0),
                                                new[:, i, :], None).then_inc(row_out[i], 16)
                    sources(r + 1)
                    for i in range(T):
                        pool.wait_ge(row_out[i], 16 * r + 16)
                    pool.sem_inc(waited, 1)
                pool.sem_inc(round_done, 1)

            @block.tensor
            def _(pe):
                pe.wait_ge(consts, 5)
                pe.wait_ge(rounds_ready, 1)
                n_rounds = pe.value_load(rounds[0:1, 0:1], min_val=1, max_val=COLS // 8)

                with pe.Fori(0, n_rounds) as r:
                    pe.wait_ge(decoded, r + 1)
                    pe.sem_inc(waited, 1)
                    for i in range(T):
                        mm = pe.transpose(ps_same[:, i, :], tgt_f[:, i:i + 1].to_broadcast([P, P]), ident[:])
                    mm.then_inc(same_ready, 1)
                    pe.wait_ge(differ_ready, r + 1)
                    for i in range(T):
                        if i >= BANKS:
                            pe.wait_ge(best_kept, T * r + i - BANKS + 1)
                        pe.wait_ge(src_in[i], 16 * r + 16)
                        pe.matmul(ps_best[i % BANKS][:], ident_b[:], differ[:, i, :].unsqueeze(1).to_broadcast([P, H, P]),
                                  start=True, stop=False, skip_group_check=True)
                        for h in range(H):
                            mm = pe.matmul(ps_best[i % BANKS][:, h, :], src_row[:, i, h:h + 1].to_broadcast([P, P]),
                                           ident[:], start=False, stop=True, skip_group_check=True)
                        mm.then_inc(best_ready, 1)
                    pe.wait_ge(load_ready, r + 1)
                    for i in range(T):
                        mm = pe.matmul(ps_sum[:, i, :], same[:, i, :], load[:, i, :], start=True, stop=True)
                    mm.then_inc(sum_ready, 1)
                pe.wait_ge(gate_ready, 1)
                for g in range(HI // 4):
                    pe.wait_ge(gate_kept, g + 1)
                    for t in range(4):
                        mm = pe.transpose(ps_gate[g % 2][:, t, :], gate[:, 4 * g + t, :], ident[:])
                    mm.then_inc(gate_turned, 1)

            @block.scalar
            def _(act):
                act.wait_ge(args_ready, 1)
                act.activation(wts[:], raw[:, 0:2, :, :], ACT.Exp).then_inc(exps_ready, 1)
                act.wait_ge(rounds_ready, 1)
                n_rounds = act.value_load(rounds[0:1, 0:1], min_val=1, max_val=COLS // 8)
                with act.Fori(0, n_rounds) as r:
                    act.wait_ge(d_ready, r + 1)
                    act.activation(load[:, :, 0:H], d[:, 0, :, :], ACT.Exp)
                    act.activation(fade[:], d[:, 1, :, :], ACT.Exp).then_inc(w_ready, 1)
                act.wait_ge(share_arg, 1)
                act.activation(share[:], zt[:, 0:T, :, :], ACT.Exp).then_inc(share_exp, 1)
                act.wait_ge(g_var, 1)
                act.activation(t2[:], t1[:], ACT.Sqrt, bias=eps[:]).then_inc(g_std, 1)
                act.wait_ge(g_arg, 1)
                act.activation(gate[:], cmp[:], ACT.Exp).then_inc(g_exp, 1)

            @block.vector
            def _(dve):
                st = Steps(dve, step)

                def do(op):
                    st.done(op)
                    st.wait()

                dve.wait_ge(params_in, 16 * 5)
                do(dve.tensor_tensor(prod[:], features[:], a_s[:].unsqueeze(1).to_broadcast([P, HI, HE]), ALU.mult))
                dve.tensor_reduce(node[:, :, 0:H], he(prod[:]), AX.X, ALU.add).then_inc(node_ready, 1)
                dve.tensor_copy(node[:, :, H:NROW], features[:]).then_inc(node_ready, 1)
                dve.wait_ge(node_ready, 2)
                do(dve.tensor_tensor(prod[:], features[:], a_d[:].unsqueeze(1).to_broadcast([P, HI, HE]), ALU.mult))
                dve.tensor_reduce(state[:, :, 0:H], he(prod[:]), AX.X, ALU.add).then_inc(node_ready, 1)
                do(dve.tensor_scalar(has[:], counts[:], 0.0, None, ALU.is_gt))
                do(dve.tensor_scalar(has_neg[:], has[:], -1.0, BIG, ALU.add, ALU.mult))
                dve.wait_ge(last_in, 16)
                tgt, own = state[:, :, 0:H], node[:, :, 0:H]
                far = last[:, 0:H].unsqueeze(1).to_broadcast([P, HI, H])
                dve.wait_ge(node_ready, 3)
                do(dve.tensor_tensor(cand[:], far, has[:].unsqueeze(2).to_broadcast([P, HI, H]), ALU.mult))
                do(dve.tensor_tensor(cand[:], cand[:], has_neg[:].unsqueeze(2).to_broadcast([P, HI, H]), ALU.add))
                do(dve.tensor_tensor(state[:, :, MX:DEN], cand[:], own, ALU.max))
                do(dve.tensor_tensor(raw[:, 0, :, :], own, tgt, ALU.add))
                do(dve.tensor_tensor(raw[:, 1, :, :], far, tgt, ALU.add))
                do(dve.tensor_tensor(raw[:, 2, :, :], state[:, :, MX:DEN], tgt, ALU.add))
                do(dve.scalar_tensor_tensor(act3[:], raw[:], SLOPE, raw[:], ALU.mult, ALU.max))
                for n in range(2):
                    do(dve.tensor_tensor(raw[:, n, :, :], act3[:, n, :, :], act3[:, 2, :, :], ALU.subtract))
                dve.tensor_scalar(raw[:, 1, :, :], raw[:, 1, :, :], 0.0, None, ALU.min).then_inc(args_ready, 1)
                dve.wait_ge(exps_ready, 1)
                do(dve.tensor_tensor(wts[:, 1, :, :], wts[:, 1, :, :], counts[:].unsqueeze(2).to_broadcast([P, HI, H]),
                                     ALU.mult))
                do(dve.tensor_tensor(state[:, :, DEN:ACC], wts[:, 0, :, :], wts[:, 1, :, :], ALU.add))
                do(dve.tensor_tensor(he(part[:]), he(features[:]), hh(wts[:, 0, :, :]), ALU.mult))
                do(dve.tensor_tensor(he(prod[:]), last[:, H:NROW].rearrange("p (h e) -> p h e", h=H).unsqueeze(1)
                                     .to_broadcast([P, HI, H, E]), hh(wts[:, 1, :, :]), ALU.mult))
                do(dve.memset(nothing[:, :, MX:DEN], -BIG))
                do(dve.memset(nothing[:, :, DEN:SROW], 0.0))
                do(dve.tensor_copy(nothing[:, :, 0:MX], state[:, :, 0:MX]))
                dve.tensor_tensor(state[:, :, ACC:SROW], part[:], prod[:], ALU.add).then_inc(state_ready, 1)
                do(dve.tensor_scalar(some[:], keys[:], 0.0, None, ALU.is_gt))
                dve.tensor_reduce(num[:], some[:], AX.X, ALU.add).then_inc(num_ready, 1)
                dve.wait_ge(num_done, 1)
                do(dve.tensor_scalar(num_i[:], num_all[:], 7.0, 8.0, ALU.add, ALU.max))
                dve.tensor_scalar(rounds[:], num_i[:], 3, None, ALU.logical_shift_right).then_inc(rounds_ready, 1)
                dve.wait_ge(consts, 4)
                do(dve.tensor_copy(spare[:], spare_i[:]))
                do(dve.tensor_copy(base[:], base_i[:]))
                dve.tensor_copy(ident_b[:], ident[:]).then_inc(consts, 1)
                dve.memset(eps[:], EPS)
                dve.wait_ge(rounds_ready, 1)
                n_rounds = dve.value_load(rounds[0:1, 0:1], min_val=1, max_val=COLS // 8)

                def find(wait_done):
                    dve.sem_inc(waited, 1)
                    wait_done(dve.max(key8[:], keys[:]))
                    dve.sem_inc(waited, 1)
                    wait_done(dve.match_replace(keys[:], key8[:], keys[:], 0.0))

                def decode(wait_done):
                    bits = key8[:].bitcast(I32)
                    dve.tensor_scalar(t_lo[:], bits, P - 1, HI_BITS, ALU.bitwise_and, ALU.logical_shift_left)
                    dve.tensor_scalar(t_hi[:], bits, LO_BITS, HI - 1, ALU.logical_shift_right, ALU.bitwise_and)
                    dve.tensor_scalar(s_lo[:], bits, NODE_BITS - HI_BITS, (P - 1) << HI_BITS,
                                      ALU.logical_shift_right, ALU.bitwise_and)
                    dve.tensor_scalar(s_hi[:], bits, NODE_BITS + LO_BITS, HI - 1,
                                      ALU.logical_shift_right, ALU.bitwise_and)
                    wait_done(dve.tensor_scalar(none8[:], key8[:], 0.0, None, ALU.is_equal))
                    dve.tensor_tensor(src_i[:], s_lo[:], s_hi[:], ALU.bitwise_or)
                    dve.tensor_scalar(spare8[:], none8[:], spare[:, 0:1], None, ALU.mult)
                    wait_done(dve.tensor_tensor(tgt0_i[:], t_lo[:], t_hi[:], ALU.bitwise_or))
                    wait_done(dve.tensor_tensor(sum8[:], tgt0_i[:], spare8[:], ALU.add))
                    wait_done(dve.tensor_tensor(tgt_f[:], sum8[:], base[:], ALU.add))
                    wait_done(dve.tensor_copy(tgt_i[:], tgt_f[:]))
                    dve.sem_inc(decoded, 1)

                find(do)
                decode(do)
                CHAIN, FOLD = 13, 4
                with dve.Fori(0, n_rounds) as r:
                    c2, c3 = Steps(dve, step2, r * CHAIN), Steps(dve, step3, r * FOLD)

                    def do2(op):
                        c2.done(op)
                        c2.wait()

                    def do3(op):
                        c3.done(op)
                        c3.wait()

                    dve.wait_ge(same_ready, r + 1)
                    do2(dve.tensor_tensor(same[:], ps_same[:], tgt_f[:].unsqueeze(2).to_broadcast([P, T, P]),
                                          ALU.is_equal))
                    dve.tensor_scalar(differ[:], same[:], -1.0, BIG, ALU.add, ALU.mult).then_inc(differ_ready, 1)
                    do2(dve.tensor_tensor(scratch[:], same[:], before[:].unsqueeze(1).to_broadcast([P, T, P]), ALU.mult))
                    dve.tensor_tensor(step_f[:], spare[:], tgt_f[:], ALU.subtract)
                    do2(dve.tensor_reduce(mates[:], scratch[:], AX.X, ALU.add))
                    do2(dve.tensor_scalar(away[:], mates[:], 0.0, None, ALU.is_gt))
                    do2(dve.tensor_tensor(away[:], away[:], step_f[:], ALU.mult))
                    do2(dve.tensor_tensor(put_f[:], away[:], tgt_f[:], ALU.add))
                    find(do2)
                    for i in range(T):
                        dve.wait_ge(best_ready, T * r + i + 1)
                        dve.tensor_reduce(best[:, i, :], ps_best[i % BANKS][:], AX.X, ALU.max).then_inc(best_kept, 1)
                    dve.wait_ge(best_kept, T * r + T)
                    dve.wait_ge(row_in, 16 * T * (r + 1))
                    dve.tensor_copy(put_i[:], put_f[:])
                    tgt1 = row[:, :, 0:H]
                    dve.tensor_copy(new[:, :, 0:H], tgt1)
                    dve.tensor_tensor(z[:, 0, :, :], src_row[:, :, 0:H], tgt1, ALU.add)
                    dve.tensor_tensor(z[:, 1, :, :], row[:, :, MX:DEN], tgt1, ALU.add)
                    do3(dve.tensor_tensor(new[:, :, MX:DEN], row[:, :, MX:DEN], best[:], ALU.max))
                    do3(dve.tensor_tensor(z[:, 2, :, :], new[:, :, MX:DEN], tgt1, ALU.add))
                    do3(dve.scalar_tensor_tensor(zl[:], z[:], SLOPE, z[:], ALU.mult, ALU.max))
                    dve.tensor_tensor(d[:], zl[:, 0:2, :, :], zl[:, 2:3, :, :].to_broadcast([P, 2, T, H]), ALU.subtract
                                      ).then_inc(d_ready, 1)
                    dve.wait_ge(w_ready, r + 1)

                    def heads(ap):
                        return ap.rearrange("p t (h e) -> p t h e", h=H)

                    dve.tensor_tensor(heads(load[:, :, H:H + HE]), heads(src_row[:, :, H:NROW]),
                                      load[:, :, 0:H].unsqueeze(3).to_broadcast([P, T, H, E]), ALU.mult
                                      ).then_inc(load_ready, 1)
                    dve.tensor_tensor(kept[:, :, 0:H], row[:, :, DEN:ACC], fade[:], ALU.mult)
                    do3(dve.tensor_tensor(heads(kept[:, :, H:H + HE]), heads(row[:, :, ACC:SROW]),
                                          fade[:].unsqueeze(3).to_broadcast([P, T, H, E]), ALU.mult))
                    dve.wait_ge(sum_ready, r + 1)
                    dve.tensor_tensor(new[:, :, DEN:SROW], kept[:], ps_sum[:], ALU.add).then_inc(new_ready, 1)
                    decode(do2)

                dve.wait_ge(state_in, 16 * T)
                maxima = tables[:, :, :, MX:DEN]
                do(dve.tensor_reduce(state[:, :, MX:DEN], maxima.rearrange("p s t h -> p t h s"), AX.X, ALU.max))
                do(dve.tensor_tensor(zt[:, 0:T, :, :], maxima, tgt.unsqueeze(1).to_broadcast([P, T, HI, H]), ALU.add))
                do(dve.tensor_tensor(zt[:, T, :, :], state[:, :, MX:DEN], tgt, ALU.add))
                do(dve.scalar_tensor_tensor(zt_l[:], zt[:], SLOPE, zt[:], ALU.mult, ALU.max))
                dve.tensor_tensor(zt[:, 0:T, :, :], zt_l[:, 0:T, :, :], zt_l[:, T:T + 1, :, :].to_broadcast([P, T, HI, H]),
                                  ALU.subtract).then_inc(share_arg, 1)
                dve.wait_ge(share_exp, 1)
                for i in range(T):
                    dve.tensor_tensor(he(tables[:, i, :, ACC:SROW]), he(tables[:, i, :, ACC:SROW]), hh(share[:, i, :, :]),
                                      ALU.mult)
                do(dve.tensor_tensor(tables[:, :, :, DEN:ACC], tables[:, :, :, DEN:ACC], share[:], ALU.mult))
                do(dve.tensor_reduce(state[:, :, DEN:SROW], tables[:, :, :, DEN:SROW].rearrange("p s t r -> p t r s"),
                                     AX.X, ALU.add))

                dve.sem_inc(gate_kept, 2)
                do(dve.tensor_scalar(g1[:], state[:, :, DEN:ACC], 1e-16, None, ALU.add))
                do(dve.reciprocal(g2[:], g1[:]))
                do(dve.tensor_tensor(he(agg[:]), he(state[:, :, ACC:SROW]), hh(g2[:]), ALU.mult))
                wide = [vec[:, n, :].unsqueeze(1).to_broadcast([P, HI, HE]) for n in range(3)]
                do(dve.tensor_tensor(agg[:], agg[:], wide[0], ALU.add))
                do(dve.tensor_reduce(t1[:], agg[:], AX.X, ALU.add))
                do(dve.tensor_scalar(t1[:], t1[:], 1.0 / HE, None, ALU.mult))
                do(dve.tensor_tensor(agg[:], agg[:], t1[:].unsqueeze(2).to_broadcast([P, HI, HE]), ALU.subtract))
                do(dve.tensor_tensor(part[:], agg[:], agg[:], ALU.mult))
                do(dve.tensor_reduce(t1[:], part[:], AX.X, ALU.add))
                dve.tensor_scalar(t1[:], t1[:], 1.0 / HE, None, ALU.mult).then_inc(g_var, 1)
                dve.wait_ge(g_std, 1)
                do(dve.reciprocal(t1[:], t2[:]))
                do(dve.tensor_tensor(agg[:], agg[:], t1[:].unsqueeze(2).to_broadcast([P, HI, HE]), ALU.mult))
                do(dve.tensor_tensor(agg[:], agg[:], wide[1], ALU.mult))
                do(dve.tensor_tensor(agg[:], agg[:], wide[2], ALU.add))
                do(dve.tensor_reduce(score[:], agg[:].rearrange("p t (h e) -> p t e h", h=H), AX.X, ALU.add))
                do(dve.tensor_scalar(score[:], score[:], 1.0 / H, None, ALU.mult))
                do(dve.memset(rank[:], 0.0))
                for e in range(E):
                    for o in range(E):
                        if o != e:
                            do(dve.tensor_tensor(cmp[:, :, 0], score[:, :, o], score[:, :, e],
                                                 ALU.is_ge if o < e else ALU.is_gt))
                            do(dve.tensor_tensor(rank[:, :, e], rank[:, :, e], cmp[:, :, 0], ALU.add))
                do(dve.tensor_reduce(t1[:], score[:], AX.X, ALU.max))
                do(dve.tensor_scalar(rank[:], rank[:], 2.0, None, ALU.is_lt))
                dve.tensor_tensor(cmp[:], score[:], t1[:].unsqueeze(2).to_broadcast([P, HI, E]), ALU.subtract
                                  ).then_inc(g_arg, 1)
                dve.wait_ge(g_exp, 1)
                do(dve.tensor_tensor(gate[:], gate[:], rank[:], ALU.mult))
                do(dve.tensor_reduce(t1[:], gate[:], AX.X, ALU.add))
                do(dve.reciprocal(t2[:], t1[:]))
                dve.tensor_tensor(gate[:], gate[:], t2[:].unsqueeze(2).to_broadcast([P, HI, E]), ALU.mult
                                  ).then_inc(gate_ready, 1)
                for g in range(HI // 4):
                    dve.wait_ge(gate_turned, g + 1)
                    dve.tensor_copy(gate_t[:, g * 4 * P:(g + 1) * 4 * P], ps_gate[g % 2].rearrange("p t n -> p (t n)")).then_inc(gate_kept, 1)


def build(nc, x4, x3, conv, gains, shifts, table, w_out, b_out, w_gat, att_src, att_dst, b_gat, gamma, beta,
          w1, b1, w2, b2, edges, out):
    def dram(name, shape):
        return nc.dram_tensor(name, shape, F32, kind="Internal").ap()

    HE = w_gat.shape[1]
    H = att_src.shape[1]
    qkv = dram("qkv", (3, B, C, N))
    attended, x_mid, tokens = (dram(n, (B, C, N)) for n in ("attended", "x_mid", "tokens"))
    node_rows = dram("node_rows", (M, H + HE))
    state_rows = dram("state_rows", (8, M + P, 3 * H + HE))
    gates = dram("gates", (w1.shape[0], M))
    with ExitStack() as ctx:
        counts = ctx.enter_context(nc.sbuf_tensor("counts", [P, HI], F32))
        keys = ctx.enter_context(nc.sbuf_tensor("keys", [P, edges.shape[1] // P], F32))
        project_and_sort(nc, x4, conv, gains, shifts, qkv, edges, counts, keys)
        attend(nc, qkv, table, attended)
        features = ctx.enter_context(nc.sbuf_tensor("features", [P, HI, HE], F32))
        mix(nc, attended, x3, w_out, b_out, w_gat, x_mid, tokens, features)
        route(nc, features, counts, keys, att_src, att_dst, b_gat, gamma, beta, node_rows, state_rows, gates)
    experts(nc, tokens, x_mid, gates.rearrange("e (b n) -> e b n", b=B), w1, b1, w2, b2, out)


def kernel(x, L0_conv_Wq, L0_conv_gq, L0_conv_bq, L0_conv_Wk, L0_conv_gk, L0_conv_bk, L0_conv_Wv, L0_conv_gv,
           L0_conv_bv, L0_conv_bias_table, L0_conv_Wout, L0_conv_bout, L0_ffn_W_gat, L0_ffn_att_src,
           L0_ffn_att_dst, L0_ffn_b_gat, L0_ffn_ln_gamma, L0_ffn_ln_beta, L0_ffn_W1, L0_ffn_b1, L0_ffn_W2,
           L0_ffn_b2, L0_ffn_edge_index):
    import concourse.bacc as _bacc
    from concourse.bass_utils import run_bass_kernel_spmd as _run

    nc = _bacc.Bacc("TRN2", target_bir_lowering=False, num_devices=1)
    arrays = {}

    def take(name, a):
        a = np.ascontiguousarray(a)
        arrays[f"in_{name}"] = a
        return nc.dram_tensor(f"in_{name}", a.shape, mybir.dt.from_np(a.dtype), kind="ExternalInput").ap()

    def by_partition(a):
        return np.asarray(a).reshape(CT, P).T

    x = np.asarray(x)
    conv = [take(f"w{n}", np.asarray(w).transpose(1, 2, 3, 0).reshape(C, TAPS, C))
            for n, w in zip("qkv", (L0_conv_Wq, L0_conv_Wk, L0_conv_Wv))]
    gains = [take(f"g{n}", by_partition(g)) for n, g in zip("qkv", (L0_conv_gq, L0_conv_gk, L0_conv_gv))]
    shifts = [take(f"b{n}", by_partition(b)) for n, b in zip("qkv", (L0_conv_bq, L0_conv_bk, L0_conv_bv))]
    x4 = take("x", x)
    x3 = x4.rearrange("b c h w -> b c (h w)")
    table = take("table", np.asarray(L0_conv_bias_table).T.reshape(HEADS, 2 * IH - 1, 2 * IW - 1))
    w_out = take("w_out", np.asarray(L0_conv_Wout)[:, :, 0, 0].T)
    b_out = take("b_out", by_partition(L0_conv_bout))
    w_gat = take("w_gat", L0_ffn_W_gat)
    att = [take(n, np.asarray(a)[None]) for n, a in (("att_src", L0_ffn_att_src), ("att_dst", L0_ffn_att_dst))]
    rows = [take(n, np.asarray(a)[None]) for n, a in
            (("b_gat", L0_ffn_b_gat), ("gamma", L0_ffn_ln_gamma), ("beta", L0_ffn_ln_beta))]
    b1 = np.asarray(L0_ffn_b1)
    w1, w2 = take("w1", L0_ffn_W1), take("w2", L0_ffn_W2)
    b1 = take("b1", b1.reshape(b1.shape[0], -1, P).transpose(2, 0, 1))
    b2 = take("b2", L0_ffn_b2)
    edges = take("edges", L0_ffn_edge_index)
    out = nc.dram_tensor("out", (B, C, N), F32, kind="ExternalOutput").ap()
    build(nc, x4, x3, conv, gains, shifts, table, w_out, b_out, w_gat, *att, *rows, w1, b1, w2, b2, edges, out)
    return _run(nc, [arrays], core_ids=[0]).results[0]["out"].reshape(x.shape)
```
